# Optimizing a Trainium2 kernel written in Bass

```python
import numpy as np
import jax
import jax.numpy as jnp

def _softmax(x, axis=-1):
    return jax.nn.softmax(x, axis=axis)

def _gelu(x):
    return jax.nn.gelu(x, approximate=True)

def _silu(x):
    return jax.nn.silu(x)

def _sigmoid(x):
    return jax.nn.sigmoid(x)

def _layernorm(x, axis=-1, eps=1e-05):
    m = jnp.mean(x, axis=axis, keepdims=True)
    v = jnp.var(x, axis=axis, keepdims=True)
    return (x - m) / jnp.sqrt(v + eps)

def _scatter_add(tgt, idx, src, axis=0):
    return tgt.at[idx].add(src)

def _segment_sum(src, seg, n):
    return jax.ops.segment_sum(src, seg, n)
kernel_name = 'mk_xattn_ffn_d1_seqx_r8_72af74'

def setup_inputs(seed: int=0):
    np.random.seed(seed)
    _w = jnp.asarray

    def _rec_inputs():
        import jax
        import jax.numpy as jnp
        _rk = jax.random.key(seed)
        x = -9.806e-05 + 1 * jax.random.normal(jax.random.fold_in(_rk, 1), (4, 512, 128), jnp.float32)
        _lenS = 512 - jax.random.randint(jax.random.fold_in(_rk, 7), (4,), 0, max(1, 512 // 4) + 1, jnp.int32)
        _lenS2 = 77 - jax.random.randint(jax.random.fold_in(_rk, 8), (4,), 0, max(1, 77 // 4) + 1, jnp.int32)
        _ctx_1024P = jax.random.normal(jax.random.fold_in(_rk, 11), (4, 16, 128), jnp.float32)
        _ctx_1024c = jax.random.dirichlet(jax.random.fold_in(_rk, 511), 0.3 * jnp.ones((16,), jnp.float32), (4, 77))
        _ctx_1024t = jnp.einsum('bsk,bkd->bsd', _ctx_1024c, _ctx_1024P)
        _ctx_1024t = _ctx_1024t * jax.lax.rsqrt(jnp.mean(jnp.square(_ctx_1024t)) + 1e-12) * 0.953939
        ctx_1024 = -1.52775e-05 + 0.999936 * (_ctx_1024t + 0.3 * jax.random.normal(jax.random.fold_in(_rk, 611), (4, 77, 128), jnp.float32))
        return (x, ctx_1024)
    x, ctx_1024 = _rec_inputs()

    def _L0_xattn_setup():
        import jax, jax.numpy as jnp
        import numpy as np
        D = 128
        NUM_ITERS = 3
        EPS = 1e-06
        SCALE = D ** (-0.5)

        def rmsnorm(x, w, eps=EPS):
            return x * jax.lax.rsqrt(jnp.mean(x * x, axis=-1, keepdims=True) + eps) * w

        def gru_cell(x, h, wih, whh, bih, bhh):
            gx = x @ wih.T + bih
            gh = h @ whh.T + bhh
            xr, xz, xn = jnp.split(gx, 3, axis=-1)
            hr, hz, hn = jnp.split(gh, 3, axis=-1)
            r = jax.nn.sigmoid(xr + hr)
            z = jax.nn.sigmoid(xz + hz)
            n = jnp.tanh(xn + r * hn)
            return (1.0 - z) * n + z * h
        key = jax.random.key(seed)
        ks = jax.random.split(key, 8)
        B, K, M, d = (8, 64, 512, D)
        w_std = d ** (-0.5)
        return {'slots': jax.random.normal(ks[0], (B, K, d), jnp.float32), 'P': jax.random.normal(ks[1], (B, M, d), jnp.float32), 'Wq': jax.random.normal(ks[2], (d, d), jnp.float32) * w_std, 'Wk': jax.random.normal(ks[3], (d, d), jnp.float32) * w_std, 'Wv': jax.random.normal(ks[4], (d, d), jnp.float32) * w_std, 'gru_wih': jax.random.normal(ks[5], (3 * d, d), jnp.float32) * w_std, 'gru_whh': jax.random.normal(ks[6], (3 * d, d), jnp.float32) * w_std, 'gru_bih': jnp.zeros((3 * d,), jnp.float32), 'gru_bhh': jnp.zeros((3 * d,), jnp.float32), 'slot_norm_w': jnp.ones((d,), jnp.float32), 'input_norm_w': jnp.ones((d,), jnp.float32)}
    _L0_xattn_all = _L0_xattn_setup()
    _L0_xattn_in = {k: v for k, v in _L0_xattn_all.items() if k in ('Wq', 'Wk', 'Wv', 'gru_wih', 'gru_whh', 'gru_bih', 'gru_bhh', 'slot_norm_w', 'input_norm_w')}
    del _L0_xattn_all

    def _L0_ffn_setup():
        import jax, jax.numpy as jnp
        import numpy as np
        TOP_K = 2

        def _gelu(x):
            return jax.nn.gelu(x, approximate=False)
        key = jax.random.key(seed)
        ks = jax.random.split(key, 6)
        B, S, D, F, E = (2, 256, 128, 256, 8)
        sc_g = 1.0 / np.sqrt(D)

        def xav(k, shape, fan_in, fan_out):
            lim = np.sqrt(6.0 / (fan_in + fan_out))
            return jax.random.uniform(k, shape, jnp.float32, -lim, lim)
        return {'x': jax.random.normal(ks[0], (B, S, D), jnp.float32), 'Wg': xav(ks[1], (D, E), D, E), 'Wu': xav(ks[2], (E, D, F), D, F), 'Wd': xav(ks[3], (E, F, D), F, D), 'W1': xav(ks[4], (D, F), D, F), 'W2': xav(ks[5], (F, D), F, D)}
    _L0_ffn_all = _L0_ffn_setup()
    _L0_ffn_in = {k: v for k, v in _L0_ffn_all.items() if k in ('Wg', 'Wu', 'Wd', 'W1', 'W2')}
    del _L0_ffn_all
    return {'x': x, 'ctx_1024': ctx_1024, 'L0_xattn_Wq': _L0_xattn_in['Wq'], 'L0_xattn_Wk': _L0_xattn_in['Wk'], 'L0_xattn_Wv': _L0_xattn_in['Wv'], 'L0_xattn_gru_wih': _L0_xattn_in['gru_wih'], 'L0_xattn_gru_whh': _L0_xattn_in['gru_whh'], 'L0_xattn_gru_bih': _L0_xattn_in['gru_bih'], 'L0_xattn_gru_bhh': _L0_xattn_in['gru_bhh'], 'L0_xattn_slot_norm_w': _L0_xattn_in['slot_norm_w'], 'L0_xattn_input_norm_w': _L0_xattn_in['input_norm_w'], 'L0_ffn_Wg': _L0_ffn_in['Wg'], 'L0_ffn_Wu': _L0_ffn_in['Wu'], 'L0_ffn_Wd': _L0_ffn_in['Wd'], 'L0_ffn_W1': _L0_ffn_in['W1'], 'L0_ffn_W2': _L0_ffn_in['W2']}

def reference(x, ctx_1024, L0_xattn_Wq, L0_xattn_Wk, L0_xattn_Wv, L0_xattn_gru_wih, L0_xattn_gru_whh, L0_xattn_gru_bih, L0_xattn_gru_bhh, L0_xattn_slot_norm_w, L0_xattn_input_norm_w, L0_ffn_Wg, L0_ffn_Wu, L0_ffn_Wd, L0_ffn_W1, L0_ffn_W2):
    import jax
    import jax.numpy as jnp

    def _L0_xattn_ref(slots, P, Wq, Wk, Wv, gru_wih, gru_whh, gru_bih, gru_bhh, slot_norm_w, input_norm_w):
        import jax, jax.numpy as jnp
        import numpy as np
        D = 128
        NUM_ITERS = 3
        EPS = 1e-06
        SCALE = D ** (-0.5)

        def rmsnorm(x, w, eps=EPS):
            return x * jax.lax.rsqrt(jnp.mean(x * x, axis=-1, keepdims=True) + eps) * w

        def gru_cell(x, h, wih, whh, bih, bhh):
            gx = x @ wih.T + bih
            gh = h @ whh.T + bhh
            xr, xz, xn = jnp.split(gx, 3, axis=-1)
            hr, hz, hn = jnp.split(gh, 3, axis=-1)
            r = jax.nn.sigmoid(xr + hr)
            z = jax.nn.sigmoid(xz + hz)
            n = jnp.tanh(xn + r * hn)
            return (1.0 - z) * n + z * h
        Pn = rmsnorm(P, input_norm_w)
        k_proj = Pn @ Wk.T
        v_proj = Pn @ Wv.T
        for _ in range(NUM_ITERS):
            sn = rmsnorm(slots, slot_norm_w)
            q_proj = sn @ Wq.T
            scores = jnp.einsum('bkd,bmd->bkm', q_proj, k_proj) * SCALE
            attn = jax.nn.softmax(scores, axis=-2)
            attn = attn / (jnp.sum(attn, axis=-1, keepdims=True) + EPS)
            updates = jnp.einsum('bkm,bmd->bkd', attn, v_proj)
            slots = gru_cell(updates, slots, gru_wih, gru_whh, gru_bih, gru_bhh)
        return slots

    def _L0_ffn_ref(x, Wg, Wu, Wd, W1, W2):
        import jax, jax.numpy as jnp
        import numpy as np
        TOP_K = 2

        def _gelu(x):
            return jax.nn.gelu(x, approximate=False)
        B, S, D = x.shape
        E = Wu.shape[0]
        T = B * S
        xt = x.reshape(T, D)
        probs = jax.nn.softmax(xt @ Wg, axis=-1)
        topv, topi = jax.lax.top_k(probs, TOP_K)
        topv = topv / jnp.sum(topv, axis=-1, keepdims=True)
        cw = jnp.zeros((T, E), x.dtype).at[jnp.arange(T)[:, None], topi].set(topv)
        h = _gelu(jnp.einsum('td,edf->tef', xt, Wu))
        y = jnp.einsum('tef,efd->ted', h, Wd)
        moe = jnp.einsum('ted,te->td', y, cw)
        shared = _gelu(xt @ W1) @ W2
        return (shared + moe).reshape(B, S, D)
    x = x + _L0_xattn_ref(_layernorm(x, axis=-1), ctx_1024, L0_xattn_Wq, L0_xattn_Wk, L0_xattn_Wv, L0_xattn_gru_wih, L0_xattn_gru_whh, L0_xattn_gru_bih, L0_xattn_gru_bhh, L0_xattn_slot_norm_w, L0_xattn_input_norm_w)
    x = x + _L0_ffn_ref(_layernorm(x, axis=-1), L0_ffn_Wg, L0_ffn_Wu, L0_ffn_Wd, L0_ffn_W1, L0_ffn_W2)
    return x

_drawn_inputs = setup_inputs


def setup_inputs(seed=0):
    import zlib

    import numpy as np

    out = dict(_drawn_inputs(seed))
    spreads = {'L0_xattn_gru_bih': (0.0, 0.1),
     'L0_xattn_gru_bhh': (0.0, 0.1),
     'L0_xattn_slot_norm_w': (1.0, 0.2),
     'L0_xattn_input_norm_w': (1.0, 0.2)}
    factors = {}
    for name, (base, spread) in spreads.items():
        noise = np.random.default_rng([zlib.crc32(name.encode()), seed]).standard_normal(out[name].shape)
        drawn = base * np.exp(spread * noise) if base else spread * noise
        out[name] = jnp.asarray(drawn.astype(out[name].dtype))
    for name, factor in factors.items():
        out[name] = (out[name] * factor).astype(out[name].dtype)
    return out
```

```python
import concourse.bass as bass
from concourse import mybir
from contextlib import ExitStack


def slot_attention_moe_kernel(nc: bass.Bass, x, ctx_in, Wq, Wk, Wv, Wih, Whh, bih, bhh,
                              slot_w, input_w, Wg, Wu, Wd, W1, W2, out):
    fp32 = mybir.dt.float32
    f32r = mybir.dt.float32r
    ALU = mybir.AluOpType
    ACT = mybir.ActivationFunctionType
    AX = mybir.AxisListType

    B, S, D = x.shape
    M = ctx_in.shape[1]
    E, _, F = Wu.shape
    P = 128
    NT = S // P
    ROUNDS = 3
    STEPS = ROUNDS * B
    LAST = STEPS - B
    SCALE = float(D) ** -0.5
    RMS_EPS, SUM_EPS, LN_EPS = 1e-6, 1e-6, 1e-5
    FH = F // P
    NF = (E + 1) * FH
    GATES = 3 * D
    NQ = 2 * NT

    ctx = ExitStack()
    with ctx:
        def sb(name, shape, dt=fp32):
            return ctx.enter_context(nc.sbuf_tensor(name, shape, dt))

        def sem(name):
            return ctx.enter_context(nc.semaphore(name))

        x_tok = sb("x_tok", [P, B * NT, D])
        ctx_tok = sb("ctx_tok", [M, B, D])
        w_nat = sb("w_nat", [P, 8, D])
        wq_nat = sb("wq_nat", [P, D])
        rows = sb("rows", [8, D])
        wg_sb = sb("wg_sb", [P, E])
        w_up = sb("w_up", [P, NF, P])
        w_down = sb("w_down", [P, NF, D])
        ident = sb("ident", [P, P])
        ones = sb("ones", [P, 1])
        sel_sum = sb("sel_sum", [2 * NQ, NQ])
        sel = sb("sel", [2 * NQ, NQ, P], f32r)
        powers = sb("powers", [P, NQ])
        earlier = sb("earlier", [P, E, E])
        w_t = sb("w_t", [P, 8, D])
        cols = sb("cols", [P, 8])
        half_b = sb("half_b", [P, 3])
        up_hi = sb("up_hi", [P, NF, P], f32r)
        up_lo = sb("up_lo", [P, NF, P], f32r)
        ctx_sq = sb("ctx_sq", [M, D])
        ctx_ss = sb("ctx_ss", [M, B])
        ctx_ms = sb("ctx_ms", [M, B])
        ctx_rms = sb("ctx_rms", [M, B])
        ctx_n = sb("ctx_n", [M, B, D])
        pn_t = sb("pn_t", [P, B * M])
        kp_t = sb("kp_t", [P, B * M])
        vp_t = sb("vp_t", [P, B * M])
        keys = sb("keys", [P, B, M])
        vals = sb("vals", [M, B, GATES])
        bn = sb("bn", [P, 2, NT, 6])
        mv = sb("mv", [P, 2, NT, 2])
        var_e = sb("var_e", [P, 2, NT])
        ln_r = sb("ln_r", [P, 2, NT])
        xn_tok = sb("xn_tok", [P, 2, NT, D])
        h_t = sb("h_t", [P, B, S])
        sq = sb("sq", [P, 2, S])
        stat = sb("stat", [P, NQ])
        fac = sb("fac", [P, NQ])
        fac_hl = sb("fac_hl", [P, 2 * NQ], f32r)
        fac_row = sb("fac_row", [2 * NQ, P], f32r)
        rms_b = sb("rms_b", [M, S])
        score = sb("score", [M, 2, S])
        smax = sb("smax", [M, 2])
        nmax = sb("nmax", [M, 2])
        expo = sb("expo", [M, 2, S])
        esum = sb("esum", [M, 2])
        rsum = sb("rsum", [M, 2])
        attn = sb("attn", [M, 2, S])
        tr = sb("tr", [P, 2, S])
        tz = sb("tz", [P, 2, S])
        hn = sb("hn", [P, 2, S])
        rn = sb("rn", [P, 2, S])
        pre = sb("pre", [P, 2, S])
        nn = sb("nn", [P, 2, S])
        diff = sb("diff", [P, 2, S])
        zd = sb("zd", [P, 2, S])
        xn_t = sb("xn_t", [P, B, S])
        xn_hi = sb("xn_hi", [P, B * S], f32r)
        xn_lo = sb("xn_lo", [P, B * S], f32r)
        lg = sb("lg", [P, 2, NT, E])
        lmax = sb("lmax", [P, 2, NT])
        ls = sb("ls", [P, 2, NT, E])
        ex = sb("ex", [P, 2, NT, E])
        gt = sb("gt", [P, 2, NT, E, E])
        eq = sb("eq", [P, 2, NT, E, E])
        tie = sb("tie", [P, 2, NT, E, E])
        ahead = sb("ahead", [P, 2, NT, E, E])
        rank = sb("rank", [P, 2, NT, E])
        top = sb("top", [P, 2, NT, E])
        tsum = sb("tsum", [P, 2, NT])
        trec = sb("trec", [P, 2, NT])
        cw = sb("cw", [P, 2, NT, E])
        cw_hl = sb("cw_hl", [P, 2, NT, 2, E], f32r)
        cw_row = sb("cw_row", [2 * E, B * S], f32r)
        RING = 3
        g = sb("g", [P, RING, S])
        gc = sb("gc", [P, RING, S])
        y_t = sb("y_t", [P, S])
        y_out = sb("y_out", [P, B * NT, D])

        bank = [ctx.enter_context(nc.psum_tensor(f"bank{i}", [P, S], fp32)) for i in range(8)]

        in_ctx, in_rows, in_w, in_x0, in_x1, in_x2, in_x3, in_wq, in_wg, in_up, in_down = (
            sem(n) for n in ("in_ctx", "in_rows", "in_w", "in_x0", "in_x1", "in_x2", "in_x3",
                             "in_wq", "in_wg", "in_up", "in_down"))
        in_x = [in_x0, in_x1, in_x2, in_x3]
        out_stored = sem("out_stored")
        zeroed, ident_ready, mask_zeroed, mask_ready = (
            sem(n) for n in ("zeroed", "ident_ready", "mask_zeroed", "mask_ready"))
        ones_ready, powers_ready, selsum_ready, sel_ready, stat_set = (
            sem(n) for n in ("ones_ready", "powers_ready", "selsum_ready", "sel_ready", "stat_set"))
        wt_done, wt_copied, cols_done, cols_copied, bias_sum, bias_ready = (
            sem(n) for n in ("wt_done", "wt_copied", "cols_done", "cols_copied", "bias_sum", "bias_ready"))
        ctx_squared, ctx_mean, ctx_rstd, ctx_scaled, ctx_turned, pn_ready = (
            sem(n) for n in ("ctx_squared", "ctx_mean", "ctx_rstd", "ctx_scaled", "ctx_turned", "pn_ready"))
        kv_done, kv_copied, keys_done, keys_ready, vals_done, vals_ready = (
            sem(n) for n in ("kv_done", "kv_copied", "keys_done", "keys_ready", "vals_done", "vals_ready"))
        up_hi_ready, up_lo_ready = sem("up_hi_ready"), sem("up_lo_ready")
        ln_stats, ln_mv, ln_var, ln_rstd, ln_scaled, ln_turned, ln_copied = (
            sem(n) for n in ("ln_stats", "ln_mv", "ln_var", "ln_rstd", "ln_scaled", "ln_turned", "ln_copied"))
        sq_ready, stats_done, stat_ready, fac_ready, fac_hi, fac_split, fac_turned, row_ready, spread = (
            sem(n) for n in ("sq_ready", "stats_done", "stat_ready", "fac_ready", "fac_hi", "fac_split",
                             "fac_turned", "row_ready", "spread"))
        scores_done, rms_copied, score_ready, nmax_ready, exp_ready, rsum_ready, attn_ready = (
            sem(n) for n in ("scores_done", "rms_copied", "score_ready", "nmax_ready", "exp_ready",
                             "rsum_ready", "attn_ready"))
        r_done, z_done, hn_done, xn_done, r_act, z_act, hn_act, n_act = (
            sem(n) for n in ("r_done", "z_done", "hn_done", "xn_done", "r_act", "z_act", "hn_act", "n_act"))
        rn_ready, pre_ready, diff_ready, zd_ready, h_ready = (
            sem(n) for n in ("rn_ready", "pre_ready", "diff_ready", "zd_ready", "h_ready"))
        h_turned, x1_ready, xn_hi_ready, xn_lo_ready, logits_done, rt, exps_ready, ranked, cw_split, cw_turned, cwrow_ready = (
            sem(n) for n in ("h_turned", "x1_ready", "xn_hi_ready", "xn_lo_ready", "logits_done", "rt",
                             "exps_ready", "ranked", "cw_split", "cw_turned", "cwrow_ready"))
        pairs, chain = sem("pairs"), sem("chain")
        up_done, cw_spread, gelu_done, scaled, down_done, y_copied, y_turned, y_added = (
            sem(n) for n in ("up_done", "cw_spread", "gelu_done", "scaled", "down_done",
                             "y_copied", "y_turned", "y_added"))

        block = ctx.enter_context(nc.Block())

        x_v = x.rearrange("b (j p) d -> p (b j) d", p=P)
        out_v = out.rearrange("b (j p) d -> b p j d", p=P)

        SMALL, SCORE, RMSB, SUMB, RB, ZB, HNB, XNB = bank
        UP = bank[0:3]
        CB = bank[3:5]
        Y, YT = bank[5], bank[6]

        @block.sync
        def _(sp):
            sp.dma_start(ctx_tok[:], ctx_in.rearrange("b m d -> m b d")).then_inc(in_ctx, 16)
            sp.dma_start(rows[0:3, :], bih.rearrange("(a d) -> a d", d=D)).then_inc(in_rows, 16)
            sp.dma_start(rows[3:6, :], bhh.rearrange("(a d) -> a d", d=D)).then_inc(in_rows, 16)
            sp.dma_start(rows[6:7, :], slot_w.rearrange("(a d) -> a d", a=1)).then_inc(in_rows, 16)
            sp.dma_start(rows[7:8, :], input_w.rearrange("(a d) -> a d", a=1)).then_inc(in_rows, 16)
            for b in range(B):
                sp.dma_start(x_tok[:, b * NT:(b + 1) * NT, :], x_v[:, b * NT:(b + 1) * NT, :]).then_inc(in_x[b], 16)
            sp.dma_start(wg_sb[:], Wg).then_inc(in_wg, 16)
            sp.dma_start(w_down[:, 0:FH, :], W2.rearrange("(h f) d -> f h d", f=P)).then_inc(in_down, 16)
            sp.dma_start(w_down[:, FH:NF, :], Wd.rearrange("e (h f) d -> f (e h) d", f=P)).then_inc(in_down, 16)
            for c in range(B):
                sp.wait_ge(y_added, c + 1)
                sp.dma_start(out_v[c], y_out[:, c * NT:(c + 1) * NT, :]).then_inc(out_stored, 16)
            sp.wait_ge(out_stored, 16 * B)

        @block.gpsimd
        def _(pool):
            nc.gpsimd.memset(ident[:], 0.0).then_inc(zeroed, 1)
            pool.wait_ge(zeroed, 1)
            nc.gpsimd.affine_select(out=ident[:], in_=ident[:], compare_op=ALU.not_equal, fill=1.0, base=0,
                                    pattern=[[-1, P]], channel_multiplier=1).then_inc(ident_ready, 1)
            nc.gpsimd.memset(earlier[:], 1.0).then_inc(mask_zeroed, 1)
            pool.wait_ge(mask_zeroed, 1)
            nc.gpsimd.affine_select(out=earlier[:], in_=earlier[:], compare_op=ALU.is_gt, fill=0.0, base=0,
                                    pattern=[[1, E], [-1, E]], channel_multiplier=0).then_inc(mask_ready, 1)
            pool.wait_ge(powers_ready, 2)
            pool.wait_ge(ctx_mean, 1)
            nc.gpsimd.tensor_tensor(ctx_rms[:], ctx_ms[:], powers[0:M, 0:B], ALU.pow).then_inc(ctx_rstd, 1)

            def ln_pow(n):
                pool.wait_ge(ln_var, n + 1)
                if n >= 2:
                    pool.wait_ge(ln_scaled, n - 1)
                nc.gpsimd.tensor_tensor(ln_r[:, n % 2, :], var_e[:, n % 2, :], powers[:, 0:NT],
                                        ALU.pow).then_inc(ln_rstd, 1)

            for b in range(B):
                ln_pow(b)
            pool.wait_ge(in_up, 32)
            nc.gpsimd.tensor_copy(up_hi[:], w_up[:]).then_inc(up_hi_ready, 1)
            pool.wait_ge(up_hi_ready, 1)
            nc.gpsimd.tensor_tensor(up_lo[:], w_up[:], up_hi[:].bitcast(fp32), ALU.subtract).then_inc(up_lo_ready, 1)

            def body(k, b, lo):
                if lo is None or lo >= 1:
                    p = (b - 1) % 2
                    pool.wait_ge(n_act, k)
                    nc.gpsimd.tensor_tensor(diff[:, p, :], h_t[:, (b - 1) % B, :], nn[:, p, :],
                                            ALU.subtract).then_inc(diff_ready, 1)
                if lo is None or lo <= STEPS - 2:
                    pool.wait_ge(stat_ready, k + 3)
                    if lo is None or lo > -2:
                        pool.wait_ge(fac_split, k + 2)
                    nc.gpsimd.tensor_tensor(fac[:], stat[:], powers[:], ALU.pow).then_inc(fac_ready, 1)

            for k in range(-2, 1):
                body(k, k % B, k)
            with pool.Fori(1, LAST + 1, B) as i:
                for j in range(B):
                    body(i + j, (1 + j) % B, None)
            for k in range(LAST + 1, STEPS + 1):
                body(k, k % B, k)

            for b in range(B):
                ln_pow(B + b)
                pool.wait_ge(xn_hi_ready, b + 1)
                nc.gpsimd.tensor_tensor(xn_lo[:, b * S:(b + 1) * S], xn_t[:, b, :],
                                        xn_hi[:, b * S:(b + 1) * S].bitcast(fp32),
                                        ALU.subtract).then_inc(xn_lo_ready, 1)

        @block.scalar
        def _(act):
            act.dma_start(w_nat[:, 0, :], Wk).then_inc(in_w, 16)
            act.dma_start(w_nat[:, 1, :], Wv).then_inc(in_w, 16)
            act.dma_start(w_nat[:, 2:5, :], Wih.rearrange("(a p) d -> p a d", p=P)).then_inc(in_w, 16)
            act.dma_start(w_nat[:, 5:8, :], Whh.rearrange("(a p) d -> p a d", p=P)).then_inc(in_w, 16)
            act.dma_start(wq_nat[:], Wq).then_inc(in_wq, 16)
            act.dma_start(w_up[:, 0:FH, :], W1.rearrange("d (h f) -> d h f", f=P)).then_inc(in_up, 16)
            act.dma_start(w_up[:, FH:NF, :].rearrange("d (e h) f -> d e (h f)", h=FH),
                          Wu.rearrange("e d f -> d e f")).then_inc(in_up, 16)
            act.wait_ge(in_ctx, 16)
            for b in range(B):
                if b:
                    act.wait_ge(ctx_squared, b)
                nc.scalar.activation(ctx_sq[:], ctx_tok[:, b, :], ACT.Square,
                                     accum_out=ctx_ss[:, b:b + 1]).then_inc(ctx_squared, 1)
            for n in range(2):
                act.wait_ge(wt_done, n + 1)
                nc.scalar.activation(w_t[:, 4 * n:4 * n + 4, :].rearrange("p a d -> p (a d)"), bank[n][:],
                                     ACT.Copy).then_inc(wt_copied, 1)
            act.wait_ge(ctx_turned, 1)
            act.wait_ge(cols_copied, 1)
            nc.scalar.activation(pn_t[:], bank[3][:, 0:B * M], ACT.Copy, scale=cols[:, 7:8]).then_inc(pn_ready, 1)
            for n, dst in enumerate((kp_t, vp_t)):
                act.wait_ge(kv_done, n + 1)
                nc.scalar.activation(dst[:], bank[6 + n][:, 0:B * M], ACT.Copy).then_inc(kv_copied, 1)

            def square(s, b, lo):
                if lo is None or lo >= B:
                    act.wait_ge(h_ready, s - B + 1)
                else:
                    act.wait_ge(ln_copied, s + 1)
                if lo is None or lo >= 2:
                    act.wait_ge(stats_done, s - 1)
                nc.scalar.activation(sq[:, b % 2, :], h_t[:, b, :], ACT.Square).then_inc(sq_ready, 1)

            for b in range(B):
                act.wait_ge(ln_turned, b + 1)
                nc.scalar.activation(h_t[:, b, :], bank[4 + b % 2][:], ACT.Copy).then_inc(ln_copied, 1)
            square(0, 0, 0)
            for b in range(B):
                act.wait_ge(vals_done, b + 1)
                nc.scalar.activation(vals[:, b, :], bank[(0, 1, 6, 7)[b]][0:M, 0:GATES], ACT.Copy).then_inc(vals_ready, 1)

            def body(k, b, lo):
                on = lambda first, last: lo is None or first <= lo <= last
                if on(1, STEPS):
                    p = (b - 1) % 2
                    act.wait_ge(pre_ready, k)
                    nc.scalar.activation(nn[:, p, :], pre[:, p, :], ACT.Tanh, bias=cols[:, 2:3]).then_inc(n_act, 1)
                if on(-1, STEPS - 2):
                    p = (b + 1) % 2
                    act.wait_ge(nmax_ready, k + 2)
                    if on(1, STEPS - 2):
                        act.wait_ge(attn_ready, k)
                        act.wait_ge(stats_done, k + 1)
                    nc.scalar.activation(expo[:, p, :], score[:, p, :], ACT.Exp, bias=nmax[:, p:p + 1],
                                         accum_out=esum[:, p:p + 1]).then_inc(exp_ready, 1)
                if on(0, STEPS - 1):
                    p = b % 2
                    act.wait_ge(r_done, k + 1)
                    nc.scalar.activation(tr[:, p, :], RB[:], ACT.Tanh, scale=0.5, bias=half_b[:, 0:1]).then_inc(r_act, 1)
                if on(-3, STEPS - 4):
                    square(k + 3, (b + 3) % B, None if lo is None else lo + 3)
                if on(0, STEPS - 1):
                    p = b % 2
                    act.wait_ge(z_done, k + 1)
                    nc.scalar.activation(tz[:, p, :], ZB[:], ACT.Tanh, scale=0.5, bias=half_b[:, 1:2]).then_inc(z_act, 1)
                    act.wait_ge(hn_done, k + 1)
                    nc.scalar.activation(hn[:, p, :], HNB[:], ACT.Identity, scale=0.5, bias=half_b[:, 2:3]).then_inc(hn_act, 1)
                if on(-2, STEPS - 3):
                    act.wait_ge(spread, k + 3)
                    if on(-1, STEPS - 3):
                        act.wait_ge(score_ready, k + 2)
                    nc.scalar.activation(rms_b[:], RMSB[0:M, :], ACT.Copy).then_inc(rms_copied, 1)

            act.wait_ge(bias_ready, 1)
            for k in range(-2, 1):
                body(k, k % B, k)
            with act.Fori(1, LAST + 1, B) as i:
                for j in range(B):
                    body(i + j, (1 + j) % B, None)
            for k in range(LAST + 1, STEPS + 1):
                body(k, k % B, k)

            for b in range(B):
                act.wait_ge(ln_turned, B + b + 1)
                nc.scalar.activation(xn_t[:, b, :], bank[2 + b % 2][:], ACT.Copy).then_inc(ln_copied, 1)
                nc.scalar.activation(xn_hi[:, b * S:(b + 1) * S], bank[2 + b % 2][:], ACT.Copy).then_inc(xn_hi_ready, 1)
                act.wait_ge(rt, 3 * b + 3)
                if b >= 2:
                    act.wait_ge(ranked, b - 1)
                nc.scalar.activation(ex[:, b % 2, :, :], ls[:, b % 2, :, :], ACT.Exp).then_inc(exps_ready, 1)

            def chunk(c, static):
                for f in range(NF):
                    act.wait_ge(up_done, NF * c + f + 1)
                    if f >= RING or static is None or static > 0:
                        act.wait_ge(down_done, NF * c + f - RING + 1)
                    nc.scalar.activation(g[:, f % RING, :], UP[f % RING][:], ACT.Gelu).then_inc(gelu_done, 1)
                act.wait_ge(down_done, NF * (c + 1))
                if static is None or static > 0:
                    act.wait_ge(y_turned, c)
                nc.scalar.activation(y_t[:], Y[:], ACT.Copy).then_inc(y_copied, 1)

            chunk(0, 0)
            with act.Fori(1, B - 1) as c:
                chunk(c, None)
            chunk(B - 1, B - 1)

        @block.vector
        def _(dve):
            nc.vector.memset(ones[:], 1.0).then_inc(ones_ready, 1)
            nc.vector.memset(powers[:, 0:NT], -0.5).then_inc(powers_ready, 1)
            nc.vector.memset(powers[:, NT:NQ], -1.0).then_inc(powers_ready, 1)
            nc.vector.memset(stat[:], 1.0).then_inc(stat_set, 1)
            dve.wait_ge(stat_set, 1)
            dve.wait_ge(ident_ready, 1)
            nc.vector.tensor_tensor(sel_sum[:], ident[0:2 * NQ, 0:NQ], ident[0:2 * NQ, NQ:2 * NQ],
                                    ALU.add).then_inc(selsum_ready, 1)
            dve.wait_ge(selsum_ready, 1)
            nc.vector.tensor_copy(sel[:], sel_sum[:].unsqueeze(2).broadcast_to([2 * NQ, NQ, P])).then_inc(sel_ready, 1)
            dve.wait_ge(ctx_squared, B)
            nc.vector.tensor_scalar(ctx_ms[:], ctx_ss[:], 1.0 / D, RMS_EPS, ALU.mult, ALU.add).then_inc(ctx_mean, 1)

            def layernorm(n, b):
                p = n % 2
                for j in range(NT):
                    nc.vector.bn_stats(bn[:, p, j, :], x_tok[:, b * NT + j, :]).then_inc(ln_stats, 1)
                for j in range(NT):
                    dve.wait_ge(ln_stats, NT * n + j + 1)
                    nc.vector.bn_aggr(mv[:, p, j, :], bn[:, p, j, :]).then_inc(ln_mv, 1)
                dve.wait_ge(ln_mv, NT * (n + 1))
                nc.vector.tensor_scalar(var_e[:, p, :], mv[:, p, :, 1], LN_EPS, None, ALU.add).then_inc(ln_var, 1)

            def normalise(n, b):
                p = n % 2
                dve.wait_ge(ln_rstd, n + 1)
                if n >= 2:
                    dve.wait_ge(ln_turned, n - 1)
                for j in range(NT):
                    last = nc.vector.tensor_scalar(xn_tok[:, p, j, :], x_tok[:, b * NT + j, :], mv[:, p, j, 0:1],
                                                   ln_r[:, p, j:j + 1], ALU.subtract, ALU.mult)
                last.then_inc(ln_scaled, 1)

            dve.wait_ge(ctx_rstd, 1)
            for b in range(B):
                last = nc.vector.tensor_scalar(ctx_n[:, b, :], ctx_tok[:, b, :], ctx_rms[:, b:b + 1], None, ALU.mult)
            last.then_inc(ctx_scaled, 1)
            dve.wait_ge(cols_done, 1)
            nc.vector.tensor_copy(cols[:], bank[2][:, 0:8]).then_inc(cols_copied, 1)
            dve.wait_ge(cols_copied, 1)
            nc.vector.tensor_tensor(half_b[:, 0:2], cols[:, 0:2], cols[:, 3:5], ALU.add).then_inc(bias_sum, 1)
            nc.vector.tensor_copy(half_b[:, 2:3], cols[:, 5:6]).then_inc(bias_sum, 1)
            dve.wait_ge(bias_sum, 2)
            nc.vector.tensor_scalar(half_b[:], half_b[:], 0.5, None, ALU.mult).then_inc(bias_ready, 1)
            dve.wait_ge(in_x[0], 16)
            layernorm(0, 0)
            for b in range(1, B):
                dve.wait_ge(in_x[b], 16)
                layernorm(b, b)
                normalise(b - 1, b - 1)
            normalise(B - 1, B - 1)
            dve.wait_ge(keys_done, 1)
            nc.vector.tensor_scalar(keys[:].rearrange("p b m -> p (b m)"), bank[3][:, 0:B * M], cols[:, 6:7], SCALE,
                                    ALU.mult, ALU.mult).then_inc(keys_ready, 1)

            def body(k, b, lo):
                on = lambda first, last: lo is None or first <= lo <= last
                if on(0, STEPS - 1):
                    p = b % 2
                    dve.wait_ge(spread, k + 2)
                    nc.vector.scalar_tensor_tensor(attn[:, p, :], expo[:, p, :], rsum[:, p:p + 1], SUMB[0:M, :],
                                                   ALU.mult, ALU.mult).then_inc(attn_ready, 1)
                if on(-1, STEPS - 2):
                    dve.wait_ge(scores_done, k + 2)
                    dve.wait_ge(rms_copied, k + 2)
                    if on(1, STEPS - 2):
                        dve.wait_ge(exp_ready, k)
                if on(1, STEPS):
                    p = (b - 1) % 2
                    dve.wait_ge(xn_done, k)
                    dve.wait_ge(rn_ready, k)
                    nc.vector.tensor_tensor(pre[:, p, :], rn[:, p, :], XNB[:], ALU.add).then_inc(pre_ready, 1)
                if on(-1, STEPS - 2):
                    p = (b + 1) % 2
                    nc.vector.tensor_tensor_reduce(out=score[:, p, :], in0=SCORE[0:M, :], in1=rms_b[:], scale=1.0,
                                                   scalar=-3.0e38, op0=ALU.mult, op1=ALU.max,
                                                   accum_out=smax[:, p:p + 1]).then_inc(score_ready, 1)
                if on(-1, STEPS - 2):
                    p = (b + 1) % 2
                    dve.wait_ge(score_ready, k + 2)
                    nc.vector.tensor_scalar(nmax[:, p:p + 1], smax[:, p:p + 1], -1.0, None, ALU.mult).then_inc(nmax_ready, 1)
                    dve.wait_ge(exp_ready, k + 2)
                    nc.vector.reciprocal(rsum[:, p:p + 1], esum[:, p:p + 1]).then_inc(rsum_ready, 1)
                if on(-2, STEPS - 2):
                    dve.wait_ge(stats_done, k + 3)
                    if on(-1, STEPS - 2):
                        dve.wait_ge(fac_ready, k + 2)
                    if on(-2, STEPS - 3):
                        last = nc.vector.tensor_scalar(stat[:, 0:NT], SMALL[:, 0:NT], 1.0 / D, RMS_EPS,
                                                       ALU.mult, ALU.add)
                    if on(-1, STEPS - 2):
                        last = nc.vector.tensor_scalar(stat[:, NT:NQ], SMALL[:, NT:NQ], SUM_EPS, None, ALU.add)
                    last.then_inc(stat_ready, 1)
                if on(1, STEPS):
                    p = (b - 1) % 2
                    dve.wait_ge(diff_ready, k)
                    dve.wait_ge(z_act, k)
                    nc.vector.scalar_tensor_tensor(zd[:, p, :], tz[:, p, :], 1.0, diff[:, p, :],
                                                   ALU.add, ALU.mult).then_inc(zd_ready, 1)
                    dve.wait_ge(zd_ready, k)
                    nc.vector.scalar_tensor_tensor(h_t[:, (b - 1) % B, :], zd[:, p, :], 0.5, nn[:, p, :],
                                                   ALU.mult, ALU.add).then_inc(h_ready, 1)
                if on(-2, STEPS - 2):
                    dve.wait_ge(fac_ready, k + 3)
                    if on(-1, STEPS - 2):
                        dve.wait_ge(fac_turned, k + 2)
                    nc.vector.tensor_copy(fac_hl[:, 0:NQ], fac[:]).then_inc(fac_hi, 1)
                    dve.wait_ge(fac_hi, k + 3)
                    nc.vector.tensor_tensor(fac_hl[:, NQ:2 * NQ], fac[:], fac_hl[:, 0:NQ].bitcast(fp32),
                                            ALU.subtract).then_inc(fac_split, 1)
                    dve.wait_ge(fac_turned, k + 3)
                    if on(-1, STEPS - 2):
                        dve.wait_ge(spread, k + 2)
                    nc.vector.tensor_copy(fac_row[:], SMALL[0:2 * NQ, P:2 * P]).then_inc(row_ready, 1)
                if on(0, STEPS - 1):
                    p = b % 2
                    dve.wait_ge(r_act, k + 1)
                    dve.wait_ge(hn_act, k + 1)
                    nc.vector.scalar_tensor_tensor(rn[:, p, :], tr[:, p, :], 1.0, hn[:, p, :],
                                                   ALU.add, ALU.mult).then_inc(rn_ready, 1)

            for k in range(-2, 1):
                body(k, k % B, k)
            with dve.Fori(1, LAST + 1, B) as i:
                for j in range(B):
                    body(i + j, (1 + j) % B, None)
            for k in range(LAST + 1, STEPS + 1):
                body(k, k % B, k)

            def residual(b):
                dve.wait_ge(h_turned, b + 1)
                nc.vector.tensor_tensor(x_tok[:, b * NT:(b + 1) * NT, :],
                                        x_tok[:, b * NT:(b + 1) * NT, :],
                                        bank[b % 2][:].rearrange("p (j d) -> p j d", d=D), ALU.add).then_inc(x1_ready, 1)
                dve.wait_ge(x1_ready, b + 1)
                layernorm(B + b, b)

            def route(b):
                p = b % 2
                n0 = 3 * b
                dve.wait_ge(logits_done, b + 1)
                nc.vector.tensor_copy(lg[:, p, :, :], bank[4][:, b * NT * E:(b + 1) * NT * E]
                                      .rearrange("p (j e) -> p j e", e=E)).then_inc(rt, 1)
                dve.wait_ge(rt, n0 + 1)
                nc.vector.reduce_max(lmax[:, p, :], lg[:, p, :, :], AX.X).then_inc(rt, 1)
                dve.wait_ge(rt, n0 + 2)
                if b >= 2:
                    dve.wait_ge(exps_ready, b - 1)
                nc.vector.tensor_tensor(ls[:, p, :, :], lg[:, p, :, :],
                                        lmax[:, p, :].unsqueeze(2).broadcast_to([P, NT, E]), ALU.subtract).then_inc(rt, 1)
                for j in range(NT):
                    own = lg[:, p, j, :].unsqueeze(2).broadcast_to([P, E, E])
                    other = lg[:, p, j, :].unsqueeze(1).broadcast_to([P, E, E])
                    nc.vector.tensor_tensor(gt[:, p, j, :, :], other, own, ALU.is_gt).then_inc(pairs, 1)
                    nc.vector.tensor_tensor(eq[:, p, j, :, :], other, own, ALU.is_equal).then_inc(pairs, 1)
                dve.wait_ge(pairs, 2 * NT * (b + 1))
                v = lambda t: t[:, p].rearrange("p j e f -> p j (e f)")
                nc.vector.tensor_tensor(v(tie), v(eq), earlier[:].rearrange("p e f -> p (e f)").unsqueeze(1)
                                        .broadcast_to([P, NT, E * E]), ALU.mult).then_inc(chain, 1)
                dve.wait_ge(chain, 7 * b + 1)
                nc.vector.tensor_tensor(v(ahead), v(tie), v(gt), ALU.add).then_inc(chain, 1)
                dve.wait_ge(chain, 7 * b + 2)
                nc.vector.reduce_sum(rank[:, p, :, :], ahead[:, p], AX.X).then_inc(chain, 1)
                dve.wait_ge(chain, 7 * b + 3)
                dve.wait_ge(exps_ready, b + 1)
                nc.vector.scalar_tensor_tensor(top[:, p, :, :], rank[:, p, :, :], 1.5, ex[:, p, :, :],
                                               ALU.is_lt, ALU.mult).then_inc(ranked, 1)
                dve.wait_ge(ranked, b + 1)
                nc.vector.reduce_sum(tsum[:, p, :], top[:, p, :, :], AX.X).then_inc(chain, 1)
                dve.wait_ge(chain, 7 * b + 4)
                nc.vector.reciprocal(trec[:, p, :], tsum[:, p, :]).then_inc(chain, 1)
                dve.wait_ge(chain, 7 * b + 5)
                nc.vector.tensor_tensor(cw[:, p, :, :], top[:, p, :, :],
                                        trec[:, p, :].unsqueeze(2).broadcast_to([P, NT, E]), ALU.mult).then_inc(chain, 1)
                dve.wait_ge(chain, 7 * b + 6)
                if b >= 2:
                    dve.wait_ge(cw_turned, b - 1)
                nc.vector.tensor_copy(cw_hl[:, p, :, 0, :], cw[:, p, :, :]).then_inc(chain, 1)
                dve.wait_ge(chain, 7 * b + 7)
                nc.vector.tensor_tensor(cw_hl[:, p, :, 1, :], cw[:, p, :, :], cw_hl[:, p, :, 0, :].bitcast(fp32),
                                        ALU.subtract).then_inc(cw_split, 1)

            def cw_rows(b):
                dve.wait_ge(cw_turned, b + 1)
                nc.vector.tensor_copy(cw_row[:, b * S:(b + 1) * S], bank[5 + b % 2][0:2 * E, :]).then_inc(cwrow_ready, 1)

            residual(0)
            for b in range(B):
                if b + 1 < B:
                    residual(b + 1)
                normalise(B + b, b)
                if b:
                    route(b - 1)
                if b > 1:
                    cw_rows(b - 2)
            route(B - 1)
            cw_rows(B - 2)
            cw_rows(B - 1)

            def chunk(c, static):
                for f in range(FH, NF):
                    e = (f - FH) // FH
                    dve.wait_ge(gelu_done, NF * c + f + 1)
                    if f % FH == 0:
                        dve.wait_ge(cw_spread, E * c + e + 1)
                    if f >= FH + RING or static is None or static > 0:
                        dve.wait_ge(down_done, NF * c + f - RING + 1)
                    nc.vector.tensor_tensor(gc[:, f % RING, :], g[:, f % RING, :], CB[e % 2][:], ALU.mult).then_inc(scaled, 1)
                    if f == FH + 3 and static != 0:
                        store(c - 1, static)

            def store(c, static):
                dve.wait_ge(y_turned, c + 1)
                nc.vector.tensor_tensor(y_out[:, bass.ds(c * NT, NT), :], x_tok[:, bass.ds(c * NT, NT), :], YT[:].rearrange("p (j d) -> p j d", d=D), ALU.add).then_inc(y_added, 1)

            chunk(0, 0)
            with dve.Fori(1, B - 1) as c:
                chunk(c, None)
            chunk(B - 1, B - 1)
            store(B - 1, B)

        @block.tensor
        def _(pe):
            pe.wait_ge(ident_ready, 1)
            pe.wait_ge(in_rows, 64)
            nc.tensor.transpose(bank[2][:, 0:8], rows[:], ident[0:8, 0:8]).then_inc(cols_done, 1)
            pe.wait_ge(in_w, 64)
            for n in range(2):
                for a in range(4):
                    last = nc.tensor.transpose(bank[n][:, a * P:(a + 1) * P], w_nat[:, 4 * n + a, :], ident[:])
                last.then_inc(wt_done, 1)
            pe.wait_ge(ctx_scaled, 1)
            for b in range(B):
                last = nc.tensor.transpose(bank[3][:, b * M:(b + 1) * M], ctx_n[:, b, :], ident[0:M, 0:M])
            last.then_inc(ctx_turned, 1)
            pe.wait_ge(pn_ready, 1)
            pe.wait_ge(wt_copied, 2)
            nc.tensor.matmul(bank[6][:, 0:B * M], w_t[:, 0, :], pn_t[:], start=True, stop=True).then_inc(kv_done, 1)
            nc.tensor.matmul(bank[7][:, 0:B * M], w_t[:, 1, :], pn_t[:], start=True, stop=True).then_inc(kv_done, 1)
            pe.wait_ge(in_wq, 16)
            pe.wait_ge(kv_copied, 1)
            nc.tensor.matmul(bank[3][:, 0:B * M], wq_nat[:], kp_t[:], start=True, stop=True).then_inc(keys_done, 1)

            def turn_norm(n, dst):
                pe.wait_ge(ln_scaled, n + 1)
                for j in range(NT):
                    last = nc.tensor.transpose(dst[:, j * P:(j + 1) * P], xn_tok[:, n % 2, j, :], ident[:])
                last.then_inc(ln_turned, 1)

            for b in range(B):
                if b >= 2:
                    pe.wait_ge(ln_copied, b - 1)
                turn_norm(b, bank[4 + b % 2])
            pe.wait_ge(kv_copied, 2)
            for b in range(B):
                nc.tensor.matmul(bank[(0, 1, 6, 7)[b]][0:M, 0:GATES], vp_t[:, b * M:(b + 1) * M],
                                 w_t[:, 2:5, :].rearrange("p a d -> p (a d)"), start=True, stop=True).then_inc(vals_done, 1)
            pe.wait_ge(ones_ready, 1)
            pe.wait_ge(sel_ready, 1)
            pe.wait_ge(keys_ready, 1)
            pe.wait_ge(ln_copied, B)
            pe.wait_ge(vals_ready, B)

            def body(k, b, lo):
                on = lambda first, last: lo is None or first <= lo <= last

                def gate(dst, n, hidden, context, done):
                    if hidden:
                        last = nc.tensor.matmul(dst[:], w_t[:, 5 + n, :], h_t[:, b, :], start=True, stop=not context)
                    if context:
                        last = nc.tensor.matmul(dst[:], vals[:, b, n * D:(n + 1) * D], attn[:, b % 2, :],
                                                start=not hidden, stop=True)
                    last.then_inc(done, 1)

                if on(0, STEPS - 1):
                    if on(1, STEPS - 1):
                        pe.wait_ge(r_act, k)
                    pe.wait_ge(attn_ready, k + 1)
                    gate(RB, 0, True, True, r_done)
                if on(-2, STEPS - 2):
                    if on(-1, STEPS - 2):
                        pe.wait_ge(row_ready, k + 2)
                    if on(-2, STEPS - 3):
                        pe.wait_ge(sq_ready, k + 3)
                        for j in range(NT):
                            last = nc.tensor.matmul(SMALL[:, j:j + 1], sq[:, b % 2, j * P:(j + 1) * P], ones[:],
                                                    start=True, stop=True)
                    if on(-1, STEPS - 2):
                        p = (b + 1) % 2
                        pe.wait_ge(rsum_ready, k + 2)
                        for j in range(NT):
                            last = nc.tensor.matmul(SMALL[:, NT + j:NT + j + 1], expo[:, p, j * P:(j + 1) * P],
                                                    rsum[:, p:p + 1], start=True, stop=True)
                    last.then_inc(stats_done, 1)
                if on(0, STEPS - 1):
                    if on(1, STEPS - 1):
                        pe.wait_ge(z_act, k)
                    gate(ZB, 1, True, True, z_done)
                    if on(1, STEPS - 1):
                        pe.wait_ge(hn_act, k)
                    gate(HNB, 2, True, False, hn_done)
                if on(-2, STEPS - 2):
                    pe.wait_ge(fac_split, k + 3)
                    nc.tensor.transpose(SMALL[0:2 * NQ, P:2 * P], fac_hl[:].bitcast(fp32), ident[:]).then_inc(fac_turned, 1)
                if on(0, STEPS - 1):
                    if on(1, STEPS - 1):
                        pe.wait_ge(pre_ready, k)
                    gate(XNB, 2, False, True, xn_done)
                if on(-2, STEPS - 2):
                    pe.wait_ge(row_ready, k + 3)
                    if on(-1, STEPS - 2):
                        pe.wait_ge(rms_copied, k + 2)
                    for j in range(NT):
                        nc.tensor.matmul(RMSB[:, j * P:(j + 1) * P], sel[:, j, :], fac_row[:], start=True, stop=True)
                    for j in range(NT):
                        last = nc.tensor.matmul(SUMB[:, j * P:(j + 1) * P], sel[:, NT + j, :], fac_row[:],
                                                start=True, stop=True)
                    last.then_inc(spread, 1)
                if on(-2, STEPS - 3):
                    if on(-1, STEPS - 3):
                        pe.wait_ge(score_ready, k + 2)
                    nc.tensor.matmul(SCORE[0:M, :], keys[:, (b + 2) % B, :], h_t[:, (b + 2) % B, :],
                                     start=True, stop=True).then_inc(scores_done, 1)

            for k in range(-2, 1):
                body(k, k % B, k)
            with pe.Fori(1, LAST + 1, B) as i:
                for j in range(B):
                    body(i + j, (1 + j) % B, None)
            for k in range(LAST + 1, STEPS):
                body(k, k % B, k)

            def turn_h(b):
                pe.wait_ge(h_ready, STEPS - B + b + 1)
                if b >= 2:
                    pe.wait_ge(x1_ready, b - 1)
                for j in range(NT):
                    last = nc.tensor.transpose(bank[b % 2][:, j * P:(j + 1) * P], h_t[:, b, j * P:(j + 1) * P], ident[:])
                last.then_inc(h_turned, 1)

            def logits(b):
                pe.wait_ge(ln_copied, B + b + 1)
                for j in range(NT):
                    at = (b * NT + j) * E
                    last = nc.tensor.matmul(bank[4][:, at:at + E], xn_t[:, b, j * P:(j + 1) * P], wg_sb[:],
                                            start=True, stop=True)
                last.then_inc(logits_done, 1)

            def turn_cw(b):
                pe.wait_ge(cw_split, b + 1)
                if b >= 2:
                    pe.wait_ge(cwrow_ready, b - 1)
                for j in range(NT):
                    last = nc.tensor.transpose(bank[5 + b % 2][0:2 * E, j * P:(j + 1) * P],
                                               cw_hl[:, b % 2, j, :, :].rearrange("p a e -> p (a e)").bitcast(fp32), ident[:])
                last.then_inc(cw_turned, 1)

            pe.wait_ge(in_wg, 16)
            turn_h(0)
            for b in range(B):
                if b + 1 < B:
                    turn_h(b + 1)
                if b >= 2:
                    pe.wait_ge(xn_hi_ready, b - 1)
                turn_norm(B + b, bank[2 + b % 2])
                if b:
                    pe.wait_ge(rt, 3 * (b - 1) + 1)
                logits(b)
                if b:
                    turn_cw(b - 1)
            turn_cw(B - 1)

            pe.wait_ge(up_hi_ready, 1)
            pe.wait_ge(up_lo_ready, 1)
            pe.wait_ge(xn_hi_ready, B)
            pe.wait_ge(xn_lo_ready, B)
            pe.wait_ge(cwrow_ready, B)
            pe.wait_ge(in_down, 32)

            def up(c, f, first):
                cols_of = bass.ds(c * S, S)
                if f >= RING or not first:
                    pe.wait_ge(gelu_done, NF * c + f - RING + 1)
                nc.tensor.matmul(UP[f % RING][:], up_hi[:, f, :], xn_lo[:, cols_of], start=True, stop=False)
                nc.tensor.matmul(UP[f % RING][:], up_lo[:, f, :], xn_hi[:, cols_of], start=False, stop=False)
                nc.tensor.matmul(UP[f % RING][:], up_hi[:, f, :], xn_hi[:, cols_of], start=False, stop=True).then_inc(up_done, 1)
                if f >= FH and f % FH == 0:
                    e = f // FH - 1
                    nc.tensor.matmul(CB[e % 2][:], sel[:, e, :], cw_row[:, cols_of], start=True, stop=True).then_inc(cw_spread, 1)

            def down(c, f, static):
                if f < FH:
                    pe.wait_ge(gelu_done, NF * c + f + 1)
                    rhs = g[:, f % RING, :]
                else:
                    pe.wait_ge(scaled, FH * E * c + f - FH + 1)
                    rhs = gc[:, f % RING, :]
                if f == 0 and static != 0:
                    pe.wait_ge(y_copied, c)
                last = nc.tensor.matmul(Y[:], w_down[:, f, :], rhs, start=f == 0, stop=f == NF - 1)
                last.then_inc(down_done, 1)

            def turn_y(c):
                pe.wait_ge(y_copied, c + 1)
                for j in range(NT):
                    last = nc.tensor.transpose(YT[:, j * P:(j + 1) * P], y_t[:, j * P:(j + 1) * P], ident[:])
                last.then_inc(y_turned, 1)

            def chunk(c, static):
                for f in range(NF):
                    if f + 2 < NF:
                        up(c, f + 2, static == 0)
                    elif static != B - 1:
                        up(c + 1, f + 2 - NF, False)
                    down(c, f, static)
                    if f == 1 and static != 0:
                        turn_y(c - 1)

            up(0, 0, True)
            up(0, 1, True)
            chunk(0, 0)
            with pe.Fori(1, B - 1) as c:
                chunk(c, None)
            chunk(B - 1, B - 1)
            turn_y(B - 1)


_INS = ['x', 'ctx_1024', 'L0_xattn_Wq', 'L0_xattn_Wk', 'L0_xattn_Wv', 'L0_xattn_gru_wih', 'L0_xattn_gru_whh',
        'L0_xattn_gru_bih', 'L0_xattn_gru_bhh', 'L0_xattn_slot_norm_w', 'L0_xattn_input_norm_w',
        'L0_ffn_Wg', 'L0_ffn_Wu', 'L0_ffn_Wd', 'L0_ffn_W1', 'L0_ffn_W2']
_OUTS = [((4, 512, 128), 'float32')]


def kernel(**inputs):
    import numpy as _np
    import concourse.bacc as _bacc
    from concourse import mybir as _mybir
    from concourse.bass_utils import run_bass_kernel_spmd as _run

    nc = _bacc.Bacc("TRN2", target_bir_lowering=False, num_devices=1)
    arrays, args = {}, []
    for name in _INS:
        a = _np.ascontiguousarray(inputs[name])
        arrays[f"in_{name}_dram"] = a
        args.append(nc.dram_tensor(f"in_{name}_dram", a.shape, _mybir.dt.from_np(a.dtype), kind="ExternalInput").ap())
    for i, (shape, dtype) in enumerate(_OUTS):
        dt = _mybir.dt.from_np(_np.dtype(dtype))
        args.append(nc.dram_tensor(f"out_{i}_dram", shape, dt, kind="ExternalOutput").ap())
    slot_attention_moe_kernel(nc, *args)
    r = _run(nc, [arrays], core_ids=[0])
    return r.results[0]["out_0_dram"]
```

```python
import concourse.bass as bass
from concourse import mybir
from contextlib import ExitStack


def slot_attention_moe_kernel(nc: bass.Bass, x, ctx_in, Wq, Wk, Wv, Wih, Whh, bih, bhh,
                              slot_w, input_w, Wg, Wu, Wd, W1, W2, out):
    fp32 = mybir.dt.float32
    f32r = mybir.dt.float32r
    ALU = mybir.AluOpType
    ACT = mybir.ActivationFunctionType
    AX = mybir.AxisListType

    B, S, D = x.shape
    M = ctx_in.shape[1]
    E, _, F = Wu.shape
    P = 128
    NT = S // P
    ROUNDS = 3
    STEPS = ROUNDS * B
    LAST = STEPS - B
    SCALE = float(D) ** -0.5
    RMS_EPS, SUM_EPS, LN_EPS = 1e-6, 1e-6, 1e-5
    FH = F // P
    NF = (E + 1) * FH
    NX = E * FH
    GATES = 3 * D
    NQ = 2 * NT
    WCOLS = 2 * NF * P
    WPART = WCOLS // LAST
    LAG = 4
    UPR, GR, HLR = 3, 3, 6
    VLOW = [0, 1, 4, 8, 12, 16]
    GLOW = [f for f in range(NF) if f not in VLOW]

    ctx = ExitStack()
    with ctx:
        def sb(name, shape, dt=fp32):
            return ctx.enter_context(nc.sbuf_tensor(name, shape, dt))

        def sem(name):
            return ctx.enter_context(nc.semaphore(name))

        def sems(names):
            return [sem(n) for n in names.split()]

        x_tok = sb("x_tok", [P, B * NT, D])
        ctx_tok = sb("ctx_tok", [M, B, D])
        wq_nat = sb("wq_nat", [P, D])
        wk_nat = sb("wk_nat", [P, D])
        wv_nat = sb("wv_nat", [P, D])
        gru_nat = sb("gru_nat", [P, 6, D])
        rows = sb("rows", [8, D])
        wg_sb = sb("wg_sb", [P, E])
        w_ffn = sb("w_ffn", [P, WCOLS])
        w_hi = sb("w_hi", [P, WCOLS], f32r)
        w_lo = sb("w_lo", [P, WCOLS], f32r)
        w_up = w_ffn[:, 0:NF * P].rearrange("p (n f) -> p n f", f=P)
        w_down = w_ffn[:, NF * P:WCOLS].rearrange("p (n d) -> p n d", d=D)
        ident = sb("ident", [P, P])
        ones = sb("ones", [P, 1])
        warm = sb("warm", [P, 1])
        sel_sum = sb("sel_sum", [2 * NQ, NQ])
        sel = sb("sel", [2 * NQ, NQ, P], f32r)
        powers = sb("powers", [P, NT])
        earlier = sb("earlier", [P, E, E])
        cols = sb("cols", [P, 8])
        half_b = sb("half_b", [P, 3])
        key_w = sb("key_w", [P, D])
        val_w = sb("val_w", [P, GATES])
        wih_t = sb("wih_t", [P, GATES])
        whh_hi = sb("whh_hi", [P, GATES], f32r)
        whh_lo = sb("whh_lo", [P, GATES], f32r)
        ctx_t = sb("ctx_t", [P, B * M])
        ctx_ss = sb("ctx_ss", [M, B])
        ctx_ms = sb("ctx_ms", [M, B])
        ctx_rms = sb("ctx_rms", [M, B])
        keys = sb("keys", [P, B * M])
        keys_hi = sb("keys_hi", [P, B * M], f32r)
        keys_lo = sb("keys_lo", [P, B * M], f32r)
        vals_hi = sb("vals_hi", [P, B, GATES], f32r)
        vals_lo = sb("vals_lo", [P, B, GATES], f32r)
        bn = sb("bn", [P, 2, NT, 6])
        mv = sb("mv", [P, 2, NT, 2])
        var_e = sb("var_e", [P, 2, NT])
        ln_r = sb("ln_r", [P, 2, NT])
        xn_tok = sb("xn_tok", [P, 2, NT, D])
        work = sb("work", [P, 10, S])
        g_hi = sb("g_hi", [P, HLR, S], f32r)
        g_lo = sb("g_lo", [P, HLR, S], f32r)
        h_t = sb("h_t", [P, B, S])
        in_hi = sb("in_hi", [P, B * S], f32r)
        in_lo = sb("in_lo", [P, B * S], f32r)
        sq = work[:, 0:2, :]
        stat = sb("stat", [P, NQ])
        fac = sb("fac", [P, NQ])
        fac_hl = sb("fac_hl", [P, 2 * NQ], f32r)
        fac_row = sb("fac_row", [2 * NQ, P], f32r)
        rms_b = sb("rms_b", [M, S])
        score = work[0:M, 2:4, :]
        smax = sb("smax", [M, 2])
        nmax = sb("nmax", [M, 2])
        expo = work[0:M, 4:6, :]
        esum = sb("esum", [M, 2])
        rsum = sb("rsum", [M, 2])
        attn = sb("attn", [M, S])
        attn_hi = g_hi[:, 0:2, :]
        attn_lo = g_lo[:, 0:2, :]
        tr = sb("tr", [P, S])
        tz = work[:, 6:8, :]
        hn = sb("hn", [P, S])
        rn = sb("rn", [P, S])
        ctx_sq = rn[0:M, :]
        pre = sb("pre", [P, S])
        nn = work[:, 8:10, :]
        diff = sb("diff", [P, S])
        zd = sb("zd", [P, S])
        xn_t = sb("xn_t", [P, S])
        lg = sb("lg", [P, NT, E])
        gt = sb("gt", [P, NT, E, E])
        eq = sb("eq", [P, NT, E, E])
        tie = sb("tie", [P, NT, E, E])
        ahead = sb("ahead", [P, NT, E, E])
        rank = sb("rank", [P, NT, E])
        top = sb("top", [P, NT, E])
        pair = sb("pair", [P, NT])
        arg = sb("arg", [P, NT, E])
        half_top = sb("half_top", [P, NT, E])
        tgap = sb("tgap", [P, NT, E])
        cw = sb("cw", [P, NT, E])
        cw_hl = sb("cw_hl", [P, NT, 2, E], f32r)
        cw_row = sb("cw_row", [2 * E, B * S], f32r)
        g = work[:, 0:GR, :]
        gc = work[:, GR:2 * GR, :]
        y_t = work[:, 8, :]
        y_out = h_t[:].rearrange("p b (j d) -> p (b j) d", d=D)

        bank = [ctx.enter_context(nc.psum_tensor(f"bank{i}", [P, S], fp32)) for i in range(8)]
        SMALL, SCORE, RMSB, SUMB, RB, ZB, HNB, XNB = bank
        VALS = [bank[4], bank[5], bank[7], bank[4]]
        T, MID, Y = bank[1], bank[2], bank[7]
        UP = [bank[0], bank[3], bank[4]]
        CB = [bank[5], bank[6]]

        in_ctx, in_rows, in_wkq, in_wv, in_wg, in_ffn, out_stored = sems(
            "in_ctx in_rows in_wkq in_wv in_wg in_ffn out_stored")
        in_gru = [sem(f"in_gru{n}") for n in range(2)]
        in_x = [sem(f"in_x{b}") for b in range(B)]
        pads_zeroed, ident_zeroed, ident_ready, mask_set, mask_ready, ones_ready, powers_ready, selsum_ready, sel_ready, fac_set = sems(
            "pads_zeroed ident_zeroed ident_ready mask_set mask_ready ones_ready powers_ready selsum_ready sel_ready fac_set")
        idle_ready, cols_done, cols_copied, bias_sum, bias_ready = sems("idle_ready cols_done cols_copied bias_sum bias_ready")
        ctx_turned, ctx_copied, ctx_squared, ctx_mean, ctx_rstd = sems(
            "ctx_turned ctx_copied ctx_squared ctx_mean ctx_rstd")
        keyw_done, keyw_ready, keys_done, keys_copied, keys_hi_ready, keys_ready = sems(
            "keyw_done keyw_ready keys_done keys_copied keys_hi_ready keys_ready")
        gru_turned, wih_ready, whh_hi_ready, whh_ready, valw_done, valw_ready = sems(
            "gru_turned wih_ready whh_hi_ready whh_ready valw_done valw_ready")
        vals_done, vals_hi_ready, vals_ready = sems("vals_done vals_hi_ready vals_ready")
        ln_stats, ln_mv, ln_var, ln_rstd, ln_scaled, ln_turned, ln_copied = sems(
            "ln_stats ln_mv ln_var ln_rstd ln_scaled ln_turned ln_copied")
        sq_ready, hi_ready, lo_ready, sq_summed, rms_arg, rms_ready, attn_summed, sum_arg, sum_ready = sems(
            "sq_ready hi_ready lo_ready sq_summed rms_arg rms_ready attn_summed sum_arg sum_ready")
        fac_hi, fac_split, fac_turned, row_ready, rms_spread, sum_spread = sems(
            "fac_hi fac_split fac_turned row_ready rms_spread sum_spread")
        scores_done, rms_copied, score_ready, nmax_ready, exp_ready, rsum_ready = sems(
            "scores_done rms_copied score_ready nmax_ready exp_ready rsum_ready")
        attn_ready, attn_hi_ready, attn_split = sems("attn_ready attn_hi_ready attn_split")
        r_done, z_done, hn_done, xn_done, r_act, z_act, hn_act, n_act = sems(
            "r_done z_done hn_done xn_done r_act z_act hn_act n_act")
        rn_ready, pre_ready, diff_ready, zd_ready, h_ready, w_hi_ready, w_lo_ready = sems(
            "rn_ready pre_ready diff_ready zd_ready h_ready w_hi_ready w_lo_ready")
        h_turned, x1_ready, xn_hi_ready, xn_lo_ready, logits_done = sems(
            "h_turned x1_ready xn_hi_ready xn_lo_ready logits_done")
        route, gap_arg, gap_ready, cw_chain, cw_split, cw_turned, cwrow_ready = sems(
            "route gap_arg gap_ready cw_chain cw_split cw_turned cwrow_ready")
        up_done, cw_spread, gelu_done, scaled, g_hi_ready, v_lo_ready, g_lo_ready, down_done = sems(
            "up_done cw_spread gelu_done scaled g_hi_ready v_lo_ready g_lo_ready down_done")
        y_copied, y_turned, y_added = sems("y_copied y_turned y_added")

        block = ctx.enter_context(nc.Block())

        x_v = x.rearrange("b (j p) d -> p (b j) d", p=P)
        out_v = out.rearrange("b (j p) d -> b p j d", p=P)

        @block.sync
        def _(sp):
            sp.dma_start(x_tok[:, 0:NT, :], x_v[:, 0:NT, :]).then_inc(in_x[0], 16)
            sp.dma_start(ctx_tok[:], ctx_in.rearrange("b m d -> m b d")).then_inc(in_ctx, 16)
            sp.dma_start(rows[0:3, :], bih.rearrange("(a d) -> a d", d=D)).then_inc(in_rows, 16)
            sp.dma_start(rows[3:6, :], bhh.rearrange("(a d) -> a d", d=D)).then_inc(in_rows, 16)
            sp.dma_start(rows[6:7, :], slot_w.rearrange("(a d) -> a d", a=1)).then_inc(in_rows, 16)
            sp.dma_start(rows[7:8, :], input_w.rearrange("(a d) -> a d", a=1)).then_inc(in_rows, 16)
            for b in range(1, B):
                sp.dma_start(x_tok[:, b * NT:(b + 1) * NT, :], x_v[:, b * NT:(b + 1) * NT, :]).then_inc(in_x[b], 16)
            sp.dma_start(w_up[:, 0:FH, :], W1.rearrange("d (h f) -> d h f", f=P)).then_inc(in_ffn, 16)
            sp.dma_start(w_ffn[:, FH * P:NF * P].rearrange("d (e f) -> d e f", e=E),
                         Wu.rearrange("e d f -> d e f")).then_inc(in_ffn, 16)
            sp.dma_start(w_down[:, 0:FH, :], W2.rearrange("(h f) d -> f h d", f=P)).then_inc(in_ffn, 16)
            sp.dma_start(w_down[:, FH:NF, :], Wd.rearrange("e (h f) d -> f (e h) d", f=P)).then_inc(in_ffn, 16)
            sp.dma_start(wg_sb[:], Wg).then_inc(in_wg, 16)
            for c in range(B):
                sp.wait_ge(y_added, c + 1)
                sp.dma_start(out_v[c], y_out[:, c * NT:(c + 1) * NT, :]).then_inc(out_stored, 16)
            sp.wait_ge(out_stored, 16 * B)

        @block.gpsimd
        def _(pool):
            nc.gpsimd.memset(ident[:], 0.0).then_inc(ident_zeroed, 1)
            pool.wait_ge(ident_zeroed, 1)
            nc.gpsimd.affine_select(out=ident[:], in_=ident[:], compare_op=ALU.not_equal, fill=1.0, base=0,
                                    pattern=[[-1, P]], channel_multiplier=1).then_inc(ident_ready, 1)
            nc.gpsimd.memset(earlier[:], 1.0).then_inc(mask_set, 1)
            pool.wait_ge(mask_set, 1)
            nc.gpsimd.affine_select(out=earlier[:], in_=earlier[:], compare_op=ALU.is_gt, fill=0.0, base=0,
                                    pattern=[[1, E], [-1, E]], channel_multiplier=0).then_inc(mask_ready, 1)
            nc.gpsimd.memset(vals_hi[:].bitcast(fp32), 0.0).then_inc(pads_zeroed, 1)
            nc.gpsimd.memset(attn_hi.bitcast(fp32), 0.0).then_inc(pads_zeroed, 1)
            pool.wait_ge(powers_ready, 1)

            def ln_pow(n, slot):
                pool.wait_ge(ln_var, n + 1)
                nc.gpsimd.tensor_tensor(ln_r[:, slot, :], var_e[:, slot, :], powers[:], ALU.pow).then_inc(ln_rstd, 1)

            def low_half(s, b):
                pool.wait_ge(hi_ready, s + 1)
                nc.gpsimd.tensor_tensor(in_lo[:, b * S:(b + 1) * S], h_t[:, b, :],
                                        in_hi[:, b * S:(b + 1) * S].bitcast(fp32), ALU.subtract).then_inc(lo_ready, 1)

            def body(k, b, lo):
                on = lambda first, last: lo is None or first <= lo <= last
                if on(-2, STEPS - 3):
                    pool.wait_ge(rms_arg, k + 3)
                    nc.gpsimd.tensor_tensor(fac[:, 0:NT], stat[:, 0:NT], powers[:], ALU.pow).then_inc(rms_ready, 1)
                if on(-1, STEPS - 3):
                    if on(1, LAST):
                        pool.wait_ge(w_hi_ready, k)
                    low_half(k + 2, (b + 2) % B)
                if on(1, LAST):
                    part = bass.ds((k - 1) * WPART, WPART)
                    nc.gpsimd.tensor_tensor(w_lo[:, part], w_ffn[:, part], w_hi[:, part].bitcast(fp32),
                                            ALU.subtract).then_inc(w_lo_ready, 1)

            ln_pow(0, 0)
            ln_pow(1, 1)
            nc.gpsimd.memset(attn_lo.bitcast(fp32), 0.0).then_inc(pads_zeroed, 1)
            body(-2, (-2) % B, -2)
            low_half(0, 0)
            pool.wait_ge(ctx_mean, 1)
            nc.gpsimd.tensor_tensor(ctx_rms[:], ctx_ms[:], powers[0:M, 0:B], ALU.pow).then_inc(ctx_rstd, 1)
            nc.gpsimd.memset(vals_lo[:].bitcast(fp32), 0.0).then_inc(pads_zeroed, 1)
            ln_pow(2, 0)
            body(-1, (-1) % B, -1)
            ln_pow(3, 1)
            body(0, 0, 0)
            with pool.Fori(1, LAST - B + 2, B) as i:
                for j in range(B):
                    body(i + j, (1 + j) % B, None)
            for k in range(LAST + 1, STEPS - 1):
                body(k, k % B, k)
            ln_pow(B, 0)

            def chunk(c, static):
                for f in GLOW:
                    if f == 5 and static != B - 1:
                        ln_pow(B + c + 1, 0)
                    pool.wait_ge(g_hi_ready, NF * c + f + 1)
                    nc.gpsimd.tensor_tensor(g_lo[:, f % HLR, :], gc[:, f % GR, :], g_hi[:, f % HLR, :].bitcast(fp32),
                                            ALU.subtract).then_inc(g_lo_ready, 1)

            chunk(0, 0)
            with pool.Fori(1, B - 1) as c:
                chunk(c, None)
            chunk(B - 1, B - 1)

        @block.scalar
        def _(act):
            act.dma_start(wk_nat[:], Wk).then_inc(in_wkq, 16)
            act.dma_start(wq_nat[:], Wq).then_inc(in_wkq, 16)
            act.dma_start(gru_nat[:, 0:3, :], Wih.rearrange("(a p) d -> p a d", p=P)).then_inc(in_gru[0], 16)
            act.dma_start(wv_nat[:], Wv).then_inc(in_wv, 16)
            act.dma_start(gru_nat[:, 3:6, :], Whh.rearrange("(a p) d -> p a d", p=P)).then_inc(in_gru[1], 16)
            act.wait_ge(ones_ready, 1)
            nc.scalar.activation(warm[:], ones[:], ACT.Exp)
            act.wait_ge(ctx_turned, 1)
            nc.scalar.activation(ctx_t[:], bank[3][:, 0:B * M], ACT.Copy).then_inc(ctx_copied, 1)
            act.wait_ge(gru_turned, 1)
            nc.scalar.activation(wih_t[:], bank[4][:, 0:GATES], ACT.Copy).then_inc(wih_ready, 1)

            def first_slots(b):
                act.wait_ge(ln_turned, b + 1)
                nc.scalar.activation(h_t[:, b, :], bank[6 + b % 2][:], ACT.Copy).then_inc(ln_copied, 1)

            def square(s, b, lo):
                if lo is None or lo >= B:
                    act.wait_ge(h_ready, s - B + 1)
                else:
                    act.wait_ge(ln_copied, s + 1)
                nc.scalar.activation(sq[:, b % 2, :], h_t[:, b, :], ACT.Square).then_inc(sq_ready, 1)

            def high_half(b):
                nc.scalar.activation(in_hi[:, b * S:(b + 1) * S], h_t[:, b, :], ACT.Copy).then_inc(hi_ready, 1)

            def vals_high(b):
                act.wait_ge(vals_done, b + 1)
                nc.scalar.activation(vals_hi[0:M, b, :], VALS[b][0:M, 0:GATES], ACT.Copy,
                                     scale=ctx_rms[:, b:b + 1]).then_inc(vals_hi_ready, 1)

            def candidate(s, p):
                act.wait_ge(pre_ready, s + 1)
                nc.scalar.activation(nn[:, p, :], pre[:], ACT.Tanh, bias=cols[:, 2:3]).then_inc(n_act, 1)

            def body(k, b, lo, fill=lambda: None):
                on = lambda first, last: lo is None or first <= lo <= last
                if on(0, STEPS - 1):
                    act.wait_ge(attn_ready, k + 1)
                    nc.scalar.activation(attn_hi[0:M, b % 2, :], attn[:], ACT.Copy).then_inc(attn_hi_ready, 1)
                if on(-1, STEPS - 2):
                    p = (b + 1) % 2
                    act.wait_ge(nmax_ready, k + 2)
                    nc.scalar.activation(expo[:, p, :], score[:, p, :], ACT.Exp, bias=nmax[:, p:p + 1],
                                         scale=ctx_rms[:, (b + 1) % B:(b + 1) % B + 1],
                                         accum_out=esum[:, p:p + 1]).then_inc(exp_ready, 1)
                if on(-2, STEPS - 3):
                    high_half((b + 2) % B)
                fill()
                if on(1, STEPS - 1):
                    candidate(k - 1, (b - 1) % 2)
                if on(0, STEPS - 1):
                    if on(1, STEPS - 1):
                        act.wait_ge(rn_ready, k)
                    act.wait_ge(hn_done, k + 1)
                    nc.scalar.activation(hn[:], HNB[:], ACT.Identity, scale=0.5, bias=half_b[:, 2:3]).then_inc(hn_act, 1)
                    act.wait_ge(r_done, k + 1)
                    nc.scalar.activation(tr[:], RB[:], ACT.Tanh, scale=0.5, bias=half_b[:, 0:1]).then_inc(r_act, 1)
                    act.wait_ge(z_done, k + 1)
                    nc.scalar.activation(tz[:, b % 2, :], ZB[:], ACT.Tanh, scale=0.5, bias=half_b[:, 1:2]).then_inc(z_act, 1)
                if on(-2, STEPS - 3):
                    act.wait_ge(rms_spread, k + 3)
                    nc.scalar.activation(rms_b[:], RMSB[0:M, :], ACT.Copy).then_inc(rms_copied, 1)
                if on(0, STEPS - 4):
                    square(k + 3, (b + 3) % B, None if lo is None else lo + 3)

            def context_sums():
                act.wait_ge(in_ctx, 16)
                for b in range(B):
                    nc.scalar.activation(ctx_sq[:, b * D:(b + 1) * D], ctx_tok[:, b, :], ACT.Square,
                                         accum_out=ctx_ss[:, b:b + 1]).then_inc(ctx_squared, 1)
                first_slots(1)
                square(1, 1, 1)

            def first_values():
                act.wait_ge(pads_zeroed, 1)
                vals_high(0)
                vals_high(1)
                vals_high(2)
                first_slots(2)
                square(2, 2, 2)

            act.wait_ge(keyw_done, 1)
            act.wait_ge(cols_copied, 1)
            nc.scalar.activation(key_w[:], bank[1][:, 0:D], ACT.Copy, scale=cols[:, 7:8]).then_inc(keyw_ready, 1)
            first_slots(0)
            square(0, 0, 0)
            body(-2, (-2) % B, -2, context_sums)
            act.wait_ge(gru_turned, 2)
            nc.scalar.activation(whh_hi[:], bank[5][:, 0:GATES], ACT.Copy).then_inc(whh_hi_ready, 1)
            act.wait_ge(valw_done, 1)
            nc.scalar.activation(val_w[:], bank[3][:, 0:GATES], ACT.Copy, scale=cols[:, 7:8]).then_inc(valw_ready, 1)
            act.wait_ge(ctx_rstd, 1)
            body(-1, (-1) % B, -1, first_values)
            vals_high(3)
            act.wait_ge(pads_zeroed, 2)
            act.wait_ge(bias_ready, 1)
            body(0, 0, 0, lambda: first_slots(3))
            with act.Fori(1, LAST - B + 2, B) as i:
                for j in range(B):
                    body(i + j, (1 + j) % B, None)
            def expert_input(b):
                act.wait_ge(ln_turned, B + b + 1)
                nc.scalar.activation(xn_t[:], MID[:], ACT.Copy).then_inc(ln_copied, 1)
                nc.scalar.activation(in_hi[:, bass.ds(b * S, S)], MID[:], ACT.Copy).then_inc(xn_hi_ready, 1)

            for k in range(LAST + 1, STEPS - 1):
                body(k, k % B, k)
            body(STEPS - 1, (STEPS - 1) % B, STEPS - 1, lambda: expert_input(0))

            def gap(b):
                act.wait_ge(gap_arg, b + 1)
                nc.scalar.activation(tgap[:], arg[:], ACT.Tanh).then_inc(gap_ready, 1)

            def hidden_high(c, f, wrapped):
                if f >= FH:
                    act.wait_ge(scaled, NX * c + f - FH + 1)
                if f >= HLR or wrapped:
                    act.wait_ge(down_done, NF * c + f - HLR + 1)
                if f == 0 and not wrapped:
                    act.wait_ge(xn_done, STEPS)
                src = gc if f >= FH else g
                nc.scalar.activation(g_hi[:, f % HLR, :], src[:, f % GR, :], ACT.Copy).then_inc(g_hi_ready, 1)

            def copy_y(c):
                act.wait_ge(down_done, NF * (c + 1))
                nc.scalar.activation(y_t, Y[:], ACT.Copy).then_inc(y_copied, 1)

            def chunk(c, static):
                for f in range(NF):
                    if f == 1 and static == 0:
                        gap(0)
                    if f == 2 and static == 0:
                        candidate(STEPS - 1, (STEPS - 1) % 2)
                    if f == LAG and static != 0:
                        copy_y(c - 1)
                    if f == 9 and static != B - 1:
                        expert_input(c + 1)
                    if f == 15 and static != B - 1:
                        gap(c + 1)
                    if GR <= f < GR + FH:
                        act.wait_ge(v_lo_ready, len(VLOW) * c + f - GR + 1)
                    act.wait_ge(up_done, NF * c + f + 1)
                    nc.scalar.activation(g[:, f % GR, :], UP[f % UPR][:], ACT.Gelu).then_inc(gelu_done, 1)
                    if f:
                        if f == 1 or f == 2:
                            act.wait_ge(gelu_done, NF * c + f)
                        hidden_high(c, f - 1, static != 0)
                hidden_high(c, NF - 1, static != 0)

            chunk(0, 0)
            with act.Fori(1, B - 1) as c:
                chunk(c, None)
            chunk(B - 1, B - 1)
            copy_y(B - 1)

        @block.vector
        def _(dve):
            nc.vector.memset(w_hi[:, 0:S].bitcast(fp32), 0.0).then_inc(idle_ready, 1)
            nc.vector.memset(ones[:], 1.0).then_inc(ones_ready, 1)
            nc.vector.memset(powers[:], -0.5).then_inc(powers_ready, 1)
            nc.vector.memset(fac[:, NT:NQ], 1.0).then_inc(fac_set, 1)
            dve.wait_ge(ident_ready, 1)
            nc.vector.tensor_tensor(sel_sum[:], ident[0:2 * NQ, 0:NQ], ident[0:2 * NQ, NQ:2 * NQ],
                                    ALU.add).then_inc(selsum_ready, 1)
            dve.wait_ge(selsum_ready, 1)
            nc.vector.tensor_copy(sel[:], sel_sum[:].unsqueeze(2).broadcast_to([2 * NQ, NQ, P])).then_inc(sel_ready, 1)

            def rows_at(b, j):
                return x_tok[:, bass.ds(b * NT + j, 1), :].rearrange("p o d -> p (o d)")

            def ln_spread(slot, b):
                for j in range(NT):
                    nc.vector.bn_stats(bn[:, slot, j, :], rows_at(b, j)).then_inc(ln_stats, 1)

            def ln_gather(slot):
                for j in range(NT):
                    nc.vector.bn_aggr(mv[:, slot, j, :], bn[:, slot, j, :]).then_inc(ln_mv, 1)

            def ln_args(n, slot):
                dve.wait_ge(ln_mv, NT * (n + 1))
                nc.vector.tensor_scalar(var_e[:, slot, :], mv[:, slot, :, 1], LN_EPS, None, ALU.add).then_inc(ln_var, 1)

            def ln_stat(n, slot, b):
                ln_spread(slot, b)
                dve.wait_ge(ln_stats, NT * (n + 1))
                ln_gather(slot)
                ln_args(n, slot)

            def normalise(n, slot, b, turned):
                dve.wait_ge(ln_rstd, n + 1)
                if turned is not None:
                    dve.wait_ge(ln_turned, turned)
                for j in range(NT):
                    last = nc.vector.tensor_scalar(xn_tok[:, slot, j, :], rows_at(b, j), mv[:, slot, j, 0:1],
                                                   ln_r[:, slot, j:j + 1], ALU.subtract, ALU.mult)
                last.then_inc(ln_scaled, 1)

            dve.wait_ge(in_x[0], 16)
            ln_stat(0, 0, 0)
            normalise(0, 0, 0, None)
            dve.wait_ge(cols_done, 1)
            nc.vector.tensor_copy(cols[:], bank[2][:, 0:8]).then_inc(cols_copied, 1)
            dve.wait_ge(in_x[1], 16)
            ln_stat(1, 1, 1)

            def split_keys():
                dve.wait_ge(keys_done, 1)
                nc.vector.tensor_scalar(keys[:], bank[0][:, 0:B * M], cols[:, 6:7], SCALE,
                                        ALU.mult, ALU.mult).then_inc(keys_copied, 1)
                dve.wait_ge(keys_copied, 1)
                nc.vector.tensor_copy(keys_hi[:], keys[:]).then_inc(keys_hi_ready, 1)
                dve.wait_ge(keys_hi_ready, 1)
                nc.vector.tensor_tensor(keys_lo[:], keys[:], keys_hi[:].bitcast(fp32), ALU.subtract).then_inc(keys_ready, 1)

            def vals_low(b):
                if b == 0:
                    dve.wait_ge(pads_zeroed, 4)
                dve.wait_ge(vals_hi_ready, b + 1)
                nc.vector.scalar_tensor_tensor(vals_lo[0:M, b, :], VALS[b][0:M, 0:GATES], ctx_rms[:, b:b + 1],
                                               vals_hi[0:M, b, :].bitcast(fp32), ALU.mult, ALU.subtract).then_inc(vals_ready, 1)

            def reset(s):
                dve.wait_ge(r_act, s + 1)
                dve.wait_ge(hn_act, s + 1)
                nc.vector.scalar_tensor_tensor(rn[:], tr[:], 1.0, hn[:], ALU.add, ALU.mult).then_inc(rn_ready, 1)

            def argument(s):
                dve.wait_ge(xn_done, s + 1)
                dve.wait_ge(rn_ready, s + 1)
                nc.vector.tensor_tensor(pre[:], rn[:], XNB[:], ALU.add).then_inc(pre_ready, 1)

            def difference(s, b):
                dve.wait_ge(n_act, s + 1)
                nc.vector.tensor_tensor(diff[:], h_t[:, b, :], nn[:, b % 2, :], ALU.subtract).then_inc(diff_ready, 1)

            def scaled_difference(s, b):
                dve.wait_ge(diff_ready, s + 1)
                nc.vector.scalar_tensor_tensor(zd[:], tz[:, b % 2, :], 1.0, diff[:], ALU.add, ALU.mult).then_inc(zd_ready, 1)

            def new_slots(s, b):
                dve.wait_ge(zd_ready, s + 1)
                nc.vector.scalar_tensor_tensor(h_t[:, b, :], zd[:], 0.5, nn[:, b % 2, :],
                                               ALU.mult, ALU.add).then_inc(h_ready, 1)

            def weights_low(s, p, first):
                dve.wait_ge(attn_hi_ready, s + 1)
                if first:
                    dve.wait_ge(pads_zeroed, 3)
                nc.vector.tensor_tensor(attn_lo[0:M, p, :], attn[:], attn_hi[0:M, p, :].bitcast(fp32),
                                        ALU.subtract).then_inc(attn_split, 1)

            def weights(s, p):
                nc.vector.scalar_tensor_tensor(attn[:], expo[:, p, :], rsum[:, p:p + 1], SUMB[0:M, :],
                                               ALU.mult, ALU.mult).then_inc(attn_ready, 1)

            def body(k, b, lo, fills=()):
                on = lambda first, last: lo is None or first <= lo <= last
                fill = lambda i: fills[i]() if i < len(fills) and fills[i] else None
                if on(0, STEPS - 1):
                    dve.wait_ge(sum_spread, k + 1)
                    if on(0, STEPS - 2):
                        dve.wait_ge(scores_done, k + 2)
                        dve.wait_ge(rms_copied, k + 2)
                    weights(k, b % 2)
                if lo == -1:
                    dve.wait_ge(scores_done, 1)
                    dve.wait_ge(rms_copied, 1)
                if on(-1, STEPS - 2):
                    p = (b + 1) % 2
                    bn_ = (b + 1) % B
                    nc.vector.tensor_tensor_reduce(out=score[:, p, :], in0=SCORE[0:M, :], in1=rms_b[:], scale=1.0,
                                                   scalar=-3.0e38, op0=ALU.mult, op1=ALU.max,
                                                   accum_out=smax[:, p:p + 1]).then_inc(score_ready, 1)
                    if lo == -1:
                        dve.wait_ge(ctx_rstd, 1)
                    dve.wait_ge(score_ready, k + 2)
                    nc.vector.tensor_scalar(nmax[:, p:p + 1], smax[:, p:p + 1], ctx_rms[:, bn_:bn_ + 1], -1.0,
                                            ALU.mult, ALU.mult).then_inc(nmax_ready, 1)
                if on(1, STEPS - 1):
                    reset(k - 1)
                fill(0)
                if on(-2, STEPS - 3):
                    dve.wait_ge(sq_summed, k + 3)
                    nc.vector.tensor_scalar(stat[:, 0:NT], SMALL[:, 0:NT], 1.0 / D, RMS_EPS,
                                            ALU.mult, ALU.add).then_inc(rms_arg, 1)
                if on(1, LAST):
                    if lo is None or lo == 1:
                        dve.wait_ge(in_ffn, 64)
                    part = bass.ds((k - 1) * WPART, WPART)
                    nc.vector.tensor_scalar(w_hi[:, part], w_ffn[:, part], 1.0, None, ALU.mult).then_inc(w_hi_ready, 1)
                if on(-1, STEPS - 2):
                    p = (b + 1) % 2
                    dve.wait_ge(exp_ready, k + 2)
                    nc.vector.reciprocal(rsum[:, p:p + 1], esum[:, p:p + 1]).then_inc(rsum_ready, 1)
                if on(1, STEPS - 1):
                    argument(k - 1)
                if on(0, STEPS - 1):
                    weights_low(k, b % 2, lo == 0)
                fill(1)
                if on(-1, STEPS - 2):
                    dve.wait_ge(attn_summed, k + 2)
                    nc.vector.tensor_scalar(stat[:, NT:NQ], SMALL[:, NT:NQ], SUM_EPS, None, ALU.add).then_inc(sum_arg, 1)
                    dve.wait_ge(sum_arg, k + 2)
                    nc.vector.reciprocal(fac[:, NT:NQ], stat[:, NT:NQ]).then_inc(sum_ready, 1)
                if on(-2, STEPS - 2):
                    if on(-2, STEPS - 3):
                        dve.wait_ge(rms_ready, k + 3)
                    if on(-1, STEPS - 2):
                        dve.wait_ge(sum_ready, k + 2)
                    else:
                        dve.wait_ge(fac_set, 1)
                    nc.vector.tensor_copy(fac_hl[:, 0:NQ], fac[:]).then_inc(fac_hi, 1)
                    dve.wait_ge(fac_hi, k + 3)
                    nc.vector.tensor_tensor(fac_hl[:, NQ:2 * NQ], fac[:], fac_hl[:, 0:NQ].bitcast(fp32),
                                            ALU.subtract).then_inc(fac_split, 1)
                if on(1, STEPS - 2):
                    difference(k - 1, (b - 1) % B)
                if on(-2, STEPS - 2):
                    dve.wait_ge(fac_turned, k + 3)
                    nc.vector.tensor_copy(fac_row[:], SMALL[0:2 * NQ, P:2 * P]).then_inc(row_ready, 1)
                if on(1, STEPS - 2):
                    scaled_difference(k - 1, (b - 1) % B)
                    new_slots(k - 1, (b - 1) % B)
                fill(2)

            def context_means():
                normalise(1, 1, 1, None)
                dve.wait_ge(ctx_squared, B)
                nc.vector.tensor_scalar(ctx_ms[:], ctx_ss[:], 1.0 / D, RMS_EPS, ALU.mult, ALU.add).then_inc(ctx_mean, 1)

            split_keys()
            body(-2, (-2) % B, -2, (None, context_means))
            dve.wait_ge(in_x[2], 16)
            ln_stat(2, 0, 2)

            def second_norm():
                dve.wait_ge(whh_hi_ready, 1)
                nc.vector.tensor_tensor(whh_lo[:], bank[5][:, 0:GATES], whh_hi[:].bitcast(fp32),
                                        ALU.subtract).then_inc(whh_ready, 1)
                normalise(2, 0, 2, 1)

            def first_values():
                nc.vector.tensor_tensor(half_b[:, 0:2], cols[:, 0:2], cols[:, 3:5], ALU.add).then_inc(bias_sum, 1)
                nc.vector.tensor_copy(half_b[:, 2:3], cols[:, 5:6]).then_inc(bias_sum, 1)
                dve.wait_ge(in_x[3], 16)
                ln_spread(1, 3)
                vals_low(0)
                dve.wait_ge(bias_sum, 2)
                nc.vector.tensor_scalar(half_b[:], half_b[:], 0.5, None, ALU.mult).then_inc(bias_ready, 1)

            def last_norm():
                vals_low(3)
                normalise(3, 1, 3, 2)

            body(-1, (-1) % B, -1, (second_norm, first_values))
            dve.wait_ge(ln_stats, NT * B)
            ln_gather(1)
            vals_low(1)
            ln_args(3, 1)
            vals_low(2)
            body(0, 0, 0, (last_norm,))
            with dve.Fori(1, LAST - B + 2, B) as i:
                for j in range(B):
                    body(i + j, (1 + j) % B, None)

            def residual(b, turned=T):
                dve.wait_ge(h_turned, b + 1)
                nc.vector.tensor_tensor(x_tok[:, b * NT:(b + 1) * NT, :], x_tok[:, b * NT:(b + 1) * NT, :],
                                        turned[:].rearrange("p (j d) -> p j d", d=D), ALU.add).then_inc(x1_ready, 1)

            def input_low(b):
                dve.wait_ge(xn_hi_ready, b + 1)
                own = bass.ds(b * S, S)
                nc.vector.tensor_tensor(in_lo[:, own], xn_t[:], in_hi[:, own].bitcast(fp32),
                                        ALU.subtract).then_inc(xn_lo_ready, 1)

            ROUTE = 9

            def rank_experts(b, part):
                own = lg[:].unsqueeze(3).broadcast_to([P, NT, E, E])
                other = lg[:].unsqueeze(2).broadcast_to([P, NT, E, E])
                flat = lambda t: t[:].rearrange("p j e f -> p j (e f)")
                if part == 1:
                    sum_of_two(b)
                    return
                dve.wait_ge(logits_done, b + 1)
                nc.vector.tensor_copy(lg[:], T[:, 0:NT * E].rearrange("p (j e) -> p j e", e=E)).then_inc(route, 1)
                dve.wait_ge(route, ROUTE * b + 1)
                nc.vector.tensor_tensor(eq[:], other, own, ALU.is_equal).then_inc(route, 1)
                nc.vector.tensor_tensor(gt[:], other, own, ALU.is_gt).then_inc(route, 1)
                dve.wait_ge(route, ROUTE * b + 2)
                nc.vector.tensor_tensor(flat(tie), flat(eq), earlier[:].rearrange("p e f -> p (e f)").unsqueeze(1)
                                        .broadcast_to([P, NT, E * E]), ALU.mult).then_inc(route, 1)
                dve.wait_ge(route, ROUTE * b + 4)
                nc.vector.tensor_tensor(flat(ahead), flat(tie), flat(gt), ALU.add).then_inc(route, 1)

            def sum_of_two(b):
                dve.wait_ge(route, ROUTE * b + 5)
                nc.vector.reduce_sum(rank[:], ahead[:], AX.X).then_inc(route, 1)
                dve.wait_ge(route, ROUTE * b + 6)
                nc.vector.scalar_tensor_tensor(top[:], rank[:], 1.5, lg[:], ALU.is_lt, ALU.mult).then_inc(route, 1)
                nc.vector.tensor_scalar(half_top[:], rank[:], 1.5, 0.5, ALU.is_lt, ALU.mult).then_inc(route, 1)
                dve.wait_ge(route, ROUTE * b + 7)
                nc.vector.reduce_sum(pair[:], top[:], AX.X).then_inc(route, 1)
                dve.wait_ge(route, ROUTE * b + 9)
                nc.vector.scalar_tensor_tensor(arg[:], pair[:].unsqueeze(2).broadcast_to([P, NT, E]), -0.5, lg[:],
                                               ALU.mult, ALU.add).then_inc(gap_arg, 1)

            def weigh_experts(b, first):
                dve.wait_ge(gap_ready, b + 1)
                nc.vector.scalar_tensor_tensor(cw[:], tgap[:], 1.0, half_top[:], ALU.add, ALU.mult).then_inc(cw_chain, 1)
                dve.wait_ge(cw_chain, 2 * b + 1)
                if not first:
                    dve.wait_ge(cw_turned, b)
                nc.vector.tensor_copy(cw_hl[:, :, 0, :], cw[:]).then_inc(cw_chain, 1)
                dve.wait_ge(cw_chain, 2 * b + 2)
                nc.vector.tensor_tensor(cw_hl[:, :, 1, :], cw[:], cw_hl[:, :, 0, :].bitcast(fp32),
                                        ALU.subtract).then_inc(cw_split, 1)

            def weight_rows(b):
                dve.wait_ge(cw_turned, b + 1)
                nc.vector.tensor_scalar(cw_row[:, bass.ds(b * S, S)], MID[0:2 * E, :], 1.0, None,
                                        ALU.mult).then_inc(cwrow_ready, 1)

            def row_statistics():
                dve.wait_ge(x1_ready, 1)
                ln_spread(0, 0)

            def row_arguments():
                dve.wait_ge(ln_stats, NT * (B + 1))
                ln_gather(0)
                ln_args(B, 0)

            for k in range(LAST + 1, STEPS - 2):
                body(k, k % B, k)
            body(STEPS - 2, (STEPS - 2) % B, STEPS - 2, (lambda: residual(0, MID), row_statistics, row_arguments))
            body(STEPS - 1, (STEPS - 1) % B, STEPS - 1, (lambda: normalise(B, 0, 0, 3),))
            input_low(0)
            dve.wait_ge(mask_ready, 1)
            rank_experts(0, 0)
            rank_experts(0, 1)
            reset(STEPS - 1)
            argument(STEPS - 1)
            weigh_experts(0, True)
            difference(STEPS - 2, (STEPS - 2) % B)
            scaled_difference(STEPS - 2, (STEPS - 2) % B)
            weight_rows(0)
            new_slots(STEPS - 2, (STEPS - 2) % B)
            residual(1)

            def store(c):
                dve.wait_ge(y_turned, c + 1)
                own = bass.ds(c * NT, NT)
                nc.vector.tensor_tensor(y_out[:, own, :], x_tok[:, own, :], T[:].rearrange("p (j d) -> p j d", d=D),
                                        ALU.add).then_inc(y_added, 1)

            def low_half(c, f):
                dve.wait_ge(g_hi_ready, NF * c + f + 1)
                src = gc if f >= FH else g
                nc.vector.tensor_tensor(g_lo[:, f % HLR, :], src[:, f % GR, :], g_hi[:, f % HLR, :].bitcast(fp32),
                                        ALU.subtract).then_inc(v_lo_ready, 1)

            def between(c, f, static):
                if static != 0 and f == 8:
                    store(c - 1)
                if static == 0 and f == 8:
                    residual(2)
                if static == 0 and f == 11:
                    residual(3)
                if static == 0 and f == 3:
                    difference(STEPS - 1, (STEPS - 1) % B)
                if static == 0 and f == 4:
                    scaled_difference(STEPS - 1, (STEPS - 1) % B)
                if static == 0 and f == 5:
                    new_slots(STEPS - 1, (STEPS - 1) % B)
                if static == B - 1:
                    return
                n = B + c + 1
                if f == 0 or f == 1:
                    if f == 0:
                        dve.wait_ge(x1_ready, 2 if static == 0 else B)
                    for j in (2 * f, 2 * f + 1):
                        nc.vector.bn_stats(bn[:, 0, j, :], rows_at(c + 1, j)).then_inc(ln_stats, 1)
                if f == 2:
                    ln_gather(0)
                if f == 3:
                    ln_args(n, 0)
                if f == 6:
                    normalise(n, 0, c + 1, n)
                if f == 9:
                    input_low(c + 1)
                if f == 12:
                    rank_experts(c + 1, 0)
                if f == 13:
                    rank_experts(c + 1, 1)
                if f == 15:
                    weigh_experts(c + 1, False)
                if f == 17:
                    weight_rows(c + 1)

            def chunk(c, static):
                for f in range(NF):
                    if f >= FH:
                        e = (f - FH) // FH
                        if f == 2 and static != B - 1:
                            dve.wait_ge(ln_stats, NT * (B + c + 2))
                        if f % FH == 0:
                            dve.wait_ge(cw_spread, E * c + e + 1)
                        if f < FH + GR:
                            if static != 0:
                                prior = NF - GR + f % GR
                                if prior in VLOW:
                                    dve.wait_ge(v_lo_ready, len(VLOW) * (c - 1) + VLOW.index(prior) + 1)
                                else:
                                    dve.wait_ge(g_lo_ready, len(GLOW) * (c - 1) + GLOW.index(prior) + 1)
                        elif f - GR in VLOW:
                            dve.wait_ge(v_lo_ready, len(VLOW) * c + VLOW.index(f - GR) + 1)
                        else:
                            dve.wait_ge(g_lo_ready, len(GLOW) * c + GLOW.index(f - GR) + 1)
                        dve.wait_ge(gelu_done, NF * c + f + 1)
                        nc.vector.tensor_tensor(gc[:, f % GR, :], g[:, f % GR, :], CB[e % 2][:],
                                                ALU.mult).then_inc(scaled, 1)
                    if f - 1 in VLOW:
                        low_half(c, f - 1)
                    between(c, f, static)

            chunk(0, 0)
            with dve.Fori(1, B - 1) as c:
                chunk(c, None)
            chunk(B - 1, B - 1)
            store(B - 1)

        @block.tensor
        def _(pe):
            def split_mm(dst, w_h, w_l, a_h, a_l, start=True, stop=True):
                nc.tensor.matmul(dst, w_h, a_l, start=start, stop=False)
                nc.tensor.matmul(dst, w_l, a_h, start=False, stop=False)
                return nc.tensor.matmul(dst, w_h, a_h, start=False, stop=stop)

            def idle(dst, n):
                for _ in range(n):
                    nc.tensor.matmul(dst[:], w_hi[:, 0:P], w_hi[:, 0:S], start=True, stop=True)

            pe.wait_ge(idle_ready, 1)
            idle(bank[7], 8)
            pe.wait_ge(ident_ready, 1)
            pe.wait_ge(in_ctx, 16)
            for b in range(B):
                last = nc.tensor.transpose(bank[3][:, b * M:(b + 1) * M], ctx_tok[:, b, :], ident[0:M, 0:M])
            last.then_inc(ctx_turned, 1)
            pe.wait_ge(in_wkq, 32)
            nc.tensor.matmul(bank[1][:, 0:D], wk_nat[:], wq_nat[:], start=True, stop=True).then_inc(keyw_done, 1)
            idle(bank[7], 4)

            def turn_gru(n):
                pe.wait_ge(in_gru[n], 16)
                for a in range(3):
                    last = nc.tensor.transpose(bank[4 + n][:, a * P:(a + 1) * P], gru_nat[:, 3 * n + a, :], ident[:])
                last.then_inc(gru_turned, 1)

            def turn_norm(n, slot, dst):
                pe.wait_ge(ln_scaled, n + 1)
                for j in range(NT):
                    last = nc.tensor.transpose(dst[:, j * P:(j + 1) * P], xn_tok[:, slot, j, :], ident[:])
                last.then_inc(ln_turned, 1)

            def project_values(b):
                nc.tensor.matmul(VALS[b][0:M, 0:GATES], ctx_t[:, b * M:(b + 1) * M], val_w[:],
                                 start=True, stop=True).then_inc(vals_done, 1)

            turn_gru(0)
            pe.wait_ge(in_rows, 64)
            nc.tensor.transpose(bank[2][:, 0:8], rows[:], ident[0:8, 0:8]).then_inc(cols_done, 1)
            idle(bank[7], 3)
            turn_norm(0, 0, bank[6])
            pe.wait_ge(ctx_copied, 1)
            pe.wait_ge(keyw_ready, 1)
            nc.tensor.matmul(bank[0][:, 0:B * M], key_w[:], ctx_t[:], start=True, stop=True).then_inc(keys_done, 1)
            idle(bank[7], 4)

            def body(k, b, lo, fills=()):
                on = lambda first, last: lo is None or first <= lo <= last
                fill = lambda i: fills[i]() if i < len(fills) and fills[i] else None

                def hidden(dst, n, b, stop):
                    own = slice(b * S, (b + 1) * S)
                    cols_of = slice(n * D, (n + 1) * D)
                    return split_mm(dst[:], whh_hi[:, cols_of], whh_lo[:, cols_of], in_hi[:, own], in_lo[:, own],
                                    stop=stop)

                def scores(s):
                    n = (b + 2) % B
                    pe.wait_ge(lo_ready, s + 1)
                    split_mm(SCORE[0:M, :], keys_hi[:, n * M:(n + 1) * M], keys_lo[:, n * M:(n + 1) * M],
                             in_hi[:, n * S:(n + 1) * S], in_lo[:, n * S:(n + 1) * S]).then_inc(scores_done, 1)

                def context(dst, n, start):
                    cols_of = slice(n * D, (n + 1) * D)
                    return split_mm(dst[:], vals_hi[:, b, cols_of], vals_lo[:, b, cols_of], attn_hi[:, b % 2, :],
                                    attn_lo[:, b % 2, :], start=start)

                if on(0, STEPS - 1):
                    if on(1, STEPS - 1):
                        pe.wait_ge(z_act, k)
                    hidden(ZB, 1, b, False)
                if lo == -2:
                    pe.wait_ge(keys_copied, 1)
                if on(-2, STEPS - 3):
                    pe.wait_ge(sq_ready, k + 3)
                    for j in range(NT):
                        last = nc.tensor.matmul(SMALL[:, j:j + 1], sq[:, b % 2, j * P:(j + 1) * P], ones[:],
                                                start=True, stop=True)
                    last.then_inc(sq_summed, 1)
                if on(0, STEPS - 1):
                    if on(1, STEPS - 1):
                        pe.wait_ge(hn_act, k)
                    hidden(HNB, 2, b, True).then_inc(hn_done, 1)
                    if lo == 0:
                        pe.wait_ge(vals_ready, B)
                    hidden(RB, 0, b, False)
                fill(0)
                if on(-1, STEPS - 2):
                    p = (b + 1) % 2
                    pe.wait_ge(rsum_ready, k + 2)
                    for j in range(NT):
                        last = nc.tensor.matmul(SMALL[:, NT + j:NT + j + 1], expo[:, p, j * P:(j + 1) * P],
                                                rsum[:, p:p + 1], start=True, stop=True)
                    last.then_inc(attn_summed, 1)
                fill(1)
                if on(0, STEPS - 1):
                    pe.wait_ge(attn_split, k + 1)
                    context(RB, 0, False).then_inc(r_done, 1)
                    context(ZB, 1, False).then_inc(z_done, 1)
                if on(-2, STEPS - 2):
                    pe.wait_ge(fac_split, k + 3)
                    nc.tensor.transpose(SMALL[0:2 * NQ, P:2 * P], fac_hl[:].bitcast(fp32), ident[:]).then_inc(fac_turned, 1)
                fill(2)
                if on(0, STEPS - 3):
                    scores(k + 2)
                if on(-2, STEPS - 2):
                    pe.wait_ge(row_ready, k + 3)
                if on(-2, STEPS - 3):
                    for j in range(NT):
                        last = nc.tensor.matmul(RMSB[:, j * P:(j + 1) * P], sel[:, j, :], fac_row[:],
                                                start=True, stop=True)
                    last.then_inc(rms_spread, 1)
                if lo == -2:
                    pe.wait_ge(keys_ready, 1)
                    scores(0)
                if on(-1, STEPS - 2):
                    for j in range(NT):
                        last = nc.tensor.matmul(SUMB[:, j * P:(j + 1) * P], sel[:, NT + j, :], fac_row[:],
                                                start=True, stop=True)
                    last.then_inc(sum_spread, 1)
                if lo == -1:
                    scores(1)
                if on(0, STEPS - 1):
                    if on(1, STEPS - 1):
                        pe.wait_ge(pre_ready, k)
                    if lo == 0:
                        pe.wait_ge(ln_copied, B)
                    context(XNB, 2, True).then_inc(xn_done, 1)

            pe.wait_ge(ones_ready, 1)
            pe.wait_ge(sel_ready, 1)
            def first_values():
                pe.wait_ge(valw_ready, 1)
                pe.wait_ge(whh_ready, 1)
                for b in range(3):
                    project_values(b)

            def fourth_values():
                pe.wait_ge(vals_ready, 1)
                project_values(3)

            def fourth_slots():
                pe.wait_ge(vals_ready, 3)
                turn_norm(3, 1, bank[7])

            body(-2, (-2) % B, -2, (None, lambda: idle(bank[7], 4), lambda: turn_norm(1, 1, bank[7])))
            turn_gru(1)
            pe.wait_ge(in_wv, 16)
            pe.wait_ge(wih_ready, 1)
            nc.tensor.matmul(bank[3][:, 0:GATES], wv_nat[:], wih_t[:], start=True, stop=True).then_inc(valw_done, 1)
            idle(bank[4], 4)
            body(-1, (-1) % B, -1, (first_values, lambda: turn_norm(2, 0, bank[6]), fourth_values))
            pe.wait_ge(vals_ready, 2)
            pe.wait_ge(ln_copied, 3)
            body(0, 0, 0, (None, fourth_slots))
            with pe.Fori(1, LAST - B + 2, B) as i:
                for j in range(B):
                    body(i + j, (1 + j) % B, None)

            def turn_h(b, dst=T):
                pe.wait_ge(h_ready, STEPS - B + b + 1)
                if b == 0:
                    pe.wait_ge(rms_copied, STEPS)
                elif b == 1:
                    pe.wait_ge(route, 1)
                else:
                    pe.wait_ge(x1_ready, b)
                for j in range(NT):
                    last = nc.tensor.transpose(dst[:, j * P:(j + 1) * P], h_t[:, b, j * P:(j + 1) * P], ident[:])
                last.then_inc(h_turned, 1)

            def logits(b):
                pe.wait_ge(xn_hi_ready, b + 1)
                for j in range(NT):
                    last = nc.tensor.matmul(T[:, j * E:(j + 1) * E], xn_t[:, j * P:(j + 1) * P], wg_sb[:],
                                            start=True, stop=True)
                last.then_inc(logits_done, 1)

            def turn_weights(b):
                pe.wait_ge(cw_split, b + 1)
                for j in range(NT):
                    last = nc.tensor.transpose(MID[0:2 * E, j * P:(j + 1) * P],
                                               cw_hl[:, j, :, :].rearrange("p a e -> p (a e)").bitcast(fp32), ident[:])
                last.then_inc(cw_turned, 1)

            def up(c, f, first):
                own = bass.ds(c * S, S)
                n = slice(f * P, (f + 1) * P)
                if f == 0:
                    pe.wait_ge(xn_lo_ready, c + 1)
                if f >= FH and f % FH == 1:
                    e = f // FH - 1
                    if e == 0:
                        if not first:
                            pe.wait_ge(cwrow_ready, c + 1)
                            pe.wait_ge(scaled, NX * c)
                    else:
                        if e >= 2 or not first:
                            pe.wait_ge(scaled, NX * c + FH * (e - 1))
                if f >= UPR or not first:
                    pe.wait_ge(gelu_done, NF * c + f - UPR + 1)
                split_mm(UP[f % UPR][:], w_hi[:, n], w_lo[:, n], in_hi[:, own], in_lo[:, own]).then_inc(up_done, 1)
                if f >= FH and f % FH == 1 and not (first and f == FH + 1):
                    spread_weights(c, f // FH - 1)

            def spread_weights(c, e):
                nc.tensor.matmul(CB[e % 2][:], sel[:, e, :], cw_row[:, bass.ds(c * S, S)],
                                 start=True, stop=True).then_inc(cw_spread, 1)

            def down(c, f, static):
                if f in VLOW:
                    pe.wait_ge(v_lo_ready, len(VLOW) * c + VLOW.index(f) + 1)
                else:
                    pe.wait_ge(g_lo_ready, len(GLOW) * c + GLOW.index(f) + 1)
                if f == 0 and static != 0:
                    pe.wait_ge(y_copied, c)
                n = slice((NF + f) * P, (NF + f + 1) * P)
                split_mm(Y[:], w_hi[:, n], w_lo[:, n], g_hi[:, f % HLR, :], g_lo[:, f % HLR, :],
                         start=f == 0, stop=f == NF - 1).then_inc(down_done, 1)

            def turn_y(c):
                pe.wait_ge(y_copied, c + 1)
                for j in range(NT):
                    last = nc.tensor.transpose(T[:, j * P:(j + 1) * P], y_t[:, j * P:(j + 1) * P], ident[:])
                last.then_inc(y_turned, 1)

            def chunk(c, static):
                ahead_too = static != B - 1
                for f in range(NF):
                    if f + LAG < NF:
                        up(c, f + LAG, static == 0)
                    elif ahead_too:
                        up(c + 1, f + LAG - NF, False)
                    down(c, f, static)
                    if f == 1 and static != 0:
                        turn_y(c - 1)
                    if f == 2 and static == 0:
                        turn_h(2)
                    if f == 5 and ahead_too:
                        turn_norm(B + c + 1, 0, MID)
                    if f == 6 and static == 0:
                        turn_h(3)
                    if f == 9 and ahead_too:
                        if static == 0:
                            pe.wait_ge(x1_ready, B)
                        else:
                            pe.wait_ge(y_added, c)
                        logits(c + 1)
                    if f == 13 and ahead_too:
                        turn_weights(c + 1)

            for k in range(LAST + 1, STEPS - 2):
                body(k, k % B, k)
            turn_h(0, MID)
            body(STEPS - 2, (STEPS - 2) % B, STEPS - 2)

            def first_logits():
                pe.wait_ge(x1_ready, 1)
                turn_norm(B, 0, MID)
                pe.wait_ge(in_wg, 16)
                logits(0)

            body(STEPS - 1, (STEPS - 1) % B, STEPS - 1, (None, first_logits))
            pe.wait_ge(w_lo_ready, LAST)
            up(0, 0, True)
            up(0, 1, True)
            turn_h(1)
            pe.wait_ge(r_act, STEPS)
            up(0, 2, True)
            up(0, 3, True)
            turn_weights(0)
            pe.wait_ge(cwrow_ready, 1)
            pe.wait_ge(z_act, STEPS)
            pe.wait_ge(hn_act, STEPS)
            spread_weights(0, 0)
            pe.wait_ge(pre_ready, STEPS)
            chunk(0, 0)
            with pe.Fori(1, B - 1) as c:
                chunk(c, None)
            chunk(B - 1, B - 1)
            turn_y(B - 1)


_INS = ['x', 'ctx_1024', 'L0_xattn_Wq', 'L0_xattn_Wk', 'L0_xattn_Wv', 'L0_xattn_gru_wih', 'L0_xattn_gru_whh',
        'L0_xattn_gru_bih', 'L0_xattn_gru_bhh', 'L0_xattn_slot_norm_w', 'L0_xattn_input_norm_w',
        'L0_ffn_Wg', 'L0_ffn_Wu', 'L0_ffn_Wd', 'L0_ffn_W1', 'L0_ffn_W2']
_OUTS = [((4, 512, 128), 'float32')]


def kernel(**inputs):
    import numpy as _np
    import concourse.bacc as _bacc
    from concourse import mybir as _mybir
    from concourse.bass_utils import run_bass_kernel_spmd as _run

    nc = _bacc.Bacc("TRN2", target_bir_lowering=False, num_devices=1)
    arrays, args = {}, []
    for name in _INS:
        a = _np.ascontiguousarray(inputs[name])
        arrays[f"in_{name}_dram"] = a
        args.append(nc.dram_tensor(f"in_{name}_dram", a.shape, _mybir.dt.from_np(a.dtype), kind="ExternalInput").ap())
    for i, (shape, dtype) in enumerate(_OUTS):
        dt = _mybir.dt.from_np(_np.dtype(dtype))
        args.append(nc.dram_tensor(f"out_{i}_dram", shape, dt, kind="ExternalOutput").ap())
    slot_attention_moe_kernel(nc, *args)
    r = _run(nc, [arrays], core_ids=[0])
    return r.results[0]["out_0_dram"]
```

```python
import concourse.bass as bass
from concourse import mybir
from contextlib import ExitStack


def slot_attention_moe_kernel(nc: bass.Bass, x, ctx_in, Wq, Wk, Wv, Wih, Whh, bih, bhh,
                              slot_w, input_w, Wg, Wu, Wd, W1, W2, out):
    fp32 = mybir.dt.float32
    f32r = mybir.dt.float32r
    ALU = mybir.AluOpType
    ACT = mybir.ActivationFunctionType
    AX = mybir.AxisListType

    B, S, D = x.shape
    M = ctx_in.shape[1]
    E, _, F = Wu.shape
    P = 128
    NT = S // P
    ROUNDS = 3
    STEPS = ROUNDS * B
    LAST = STEPS - B
    SCALE = float(D) ** -0.5
    RMS_EPS, SUM_EPS, LN_EPS = 1e-6, 1e-6, 1e-5
    FH = F // P
    NF = (E + 1) * FH
    NX = E * FH
    GATES = 3 * D
    NQ = 2 * NT
    WCOLS = 2 * NF * P
    WPART = WCOLS // LAST
    ROUTE = 9
    LAG = 4
    UPR, GR, HLR = 3, 3, 6
    VLOW = [0, 1, 3, 6, 9, 13, 16, NF - 1]
    GLOW = [f for f in range(NF) if f not in VLOW]

    ctx = ExitStack()
    with ctx:
        def sb(name, shape, dt=fp32):
            return ctx.enter_context(nc.sbuf_tensor(name, shape, dt))

        def sem(name):
            return ctx.enter_context(nc.semaphore(name))

        def sems(names):
            return [sem(n) for n in names.split()]

        x_tok = sb("x_tok", [P, B * NT, D])
        ctx_tok = sb("ctx_tok", [M, B, D])
        wq_nat = sb("wq_nat", [P, D])
        wk_nat = sb("wk_nat", [P, D])
        wv_nat = sb("wv_nat", [P, D])
        gru_nat = sb("gru_nat", [P, 6, D])
        rows = sb("rows", [8, D])
        wg_sb = sb("wg_sb", [P, E])
        w_ffn = sb("w_ffn", [P, WCOLS])
        w_hi = sb("w_hi", [P, WCOLS], f32r)
        w_lo = sb("w_lo", [P, WCOLS], f32r)
        w_up = w_ffn[:, 0:NF * P].rearrange("p (n f) -> p n f", f=P)
        w_down = w_ffn[:, NF * P:WCOLS].rearrange("p (n d) -> p n d", d=D)
        ident = sb("ident", [P, P])
        ones = sb("ones", [P, 1])
        warm = sb("warm", [P, 1])
        sel_sum = sb("sel_sum", [2 * NQ, NQ])
        sel = sb("sel", [2 * NQ, NQ, P], f32r)
        powers = sb("powers", [P, NT])
        earlier = sb("earlier", [P, E, E])
        cols = sb("cols", [P, 8])
        half_b = sb("half_b", [P, 3])
        key_w = sb("key_w", [P, D])
        val_w = sb("val_w", [P, GATES])
        wih_t = sb("wih_t", [P, GATES])
        whh_hi = sb("whh_hi", [P, GATES], f32r)
        whh_lo = sb("whh_lo", [P, GATES], f32r)
        ctx_t = sb("ctx_t", [P, B * M])
        ctx_ss = sb("ctx_ss", [M, B])
        ctx_ms = sb("ctx_ms", [M, B])
        ctx_rms = sb("ctx_rms", [M, B])
        keys = sb("keys", [P, B * M])
        keys_hi = sb("keys_hi", [P, B * M], f32r)
        keys_lo = sb("keys_lo", [P, B * M], f32r)
        vals_hi = sb("vals_hi", [P, B, GATES], f32r)
        vals_lo = sb("vals_lo", [P, B, GATES], f32r)
        bn = sb("bn", [P, 2, NT, 6])
        mv = sb("mv", [P, 2, NT, 2])
        var_e = sb("var_e", [P, 2, NT])
        ln_r = sb("ln_r", [P, 2, NT])
        xn_tok = sb("xn_tok", [P, 2, NT, D])
        work = sb("work", [P, 10, S])
        g_hi = sb("g_hi", [P, HLR, S], f32r)
        g_lo = sb("g_lo", [P, HLR, S], f32r)
        h_t = sb("h_t", [P, B, S])
        in_hi = sb("in_hi", [P, B * S], f32r)
        in_lo = sb("in_lo", [P, B * S], f32r)
        sq = work[:, 0:2, :]
        stat = sb("stat", [P, NQ])
        fac = sb("fac", [P, NQ])
        fac_hl = sb("fac_hl", [P, 2 * NQ], f32r)
        fac_row = sb("fac_row", [2 * NQ, P], f32r)
        rms_b = sb("rms_b", [M, S])
        score = work[0:M, 2:4, :]
        smax = sb("smax", [M, 2])
        nmax = sb("nmax", [M, 2])
        expo = work[0:M, 4:6, :]
        esum = sb("esum", [M, 2])
        rsum = sb("rsum", [M, 2])
        attn = sb("attn", [M, S])
        attn_hi = g_hi[:, 0:2, :]
        attn_lo = g_lo[:, 0:2, :]
        tr = sb("tr", [P, S])
        tz = work[:, 6:8, :]
        hn = sb("hn", [P, S])
        rn = sb("rn", [P, S])
        ctx_sq = rn[0:M, :]
        pre = sb("pre", [P, S])
        nn = work[:, 8:10, :]
        diff = sb("diff", [P, S])
        zd = sb("zd", [P, S])
        xn_t = sb("xn_t", [P, S])
        lg = sb("lg", [P, NT, E])
        gt = sb("gt", [P, NT, E, E])
        eq = sb("eq", [P, NT, E, E])
        tie = sb("tie", [P, NT, E, E])
        ahead = sb("ahead", [P, NT, E, E])
        rank = sb("rank", [P, NT, E])
        top = sb("top", [P, NT, E])
        pair = sb("pair", [P, NT])
        arg = sb("arg", [P, NT, E])
        half_top = sb("half_top", [P, NT, E])
        tgap = sb("tgap", [P, NT, E])
        cw = sb("cw", [P, NT, E])
        cw_hl = sb("cw_hl", [P, NT, 2, E], f32r)
        cw_row = sb("cw_row", [2 * E, B * S], f32r)
        g = work[:, 0:GR, :]
        gc = work[:, GR:2 * GR, :]
        y_t = work[:, 8, :]
        y_out = h_t[:].rearrange("p b (j d) -> p (b j) d", d=D)

        bank = [ctx.enter_context(nc.psum_tensor(f"bank{i}", [P, S], fp32)) for i in range(8)]
        SMALL, SCORE, RMSB, SUMB, RB, ZB, HNB, XNB = bank
        VALS = [bank[4], bank[5], bank[7], bank[4]]
        T, MID, Y = bank[1], bank[2], bank[7]
        UP = [bank[0], bank[3], bank[4]]
        CB = [bank[5], bank[6]]

        in_ctx, in_rows, in_wkq, in_wv, in_wg, in_ffn, out_stored = sems(
            "in_ctx in_rows in_wkq in_wv in_wg in_ffn out_stored")
        in_gru = [sem(f"in_gru{n}") for n in range(2)]
        in_x = [sem(f"in_x{b}") for b in range(B)]
        pads_zeroed, ident_zeroed, ident_ready, mask_set, mask_ready, ones_ready, powers_ready = sems(
            "pads_zeroed ident_zeroed ident_ready mask_set mask_ready ones_ready powers_ready")
        selsum_ready, sel_ready, fac_set = sems("selsum_ready sel_ready fac_set")
        idle_ready, cols_done, cols_copied, bias_sum, bias_ready = sems(
            "idle_ready cols_done cols_copied bias_sum bias_ready")
        ctx_turned, ctx_copied, ctx_squared, ctx_mean, ctx_rstd = sems(
            "ctx_turned ctx_copied ctx_squared ctx_mean ctx_rstd")
        keyw_done, keyw_ready, keys_done, keys_copied, keys_hi_ready, keys_ready = sems(
            "keyw_done keyw_ready keys_done keys_copied keys_hi_ready keys_ready")
        gru_turned, wih_ready, whh_hi_ready, whh_ready, valw_done, valw_ready = sems(
            "gru_turned wih_ready whh_hi_ready whh_ready valw_done valw_ready")
        vals_done, vals_hi_ready, vals_ready = sems("vals_done vals_hi_ready vals_ready")
        ln_stats, ln_mv, ln_var, ln_rstd, ln_scaled, ln_turned, ln_copied = sems(
            "ln_stats ln_mv ln_var ln_rstd ln_scaled ln_turned ln_copied")
        sq_ready, hi_ready, lo_ready, sq_summed, rms_arg, rms_ready, attn_summed = sems(
            "sq_ready hi_ready lo_ready sq_summed rms_arg rms_ready attn_summed")
        sum_arg, sum_ready = sems("sum_arg sum_ready")
        fac_hi, fac_split, fac_turned, row_ready, rms_spread, sum_spread = sems(
            "fac_hi fac_split fac_turned row_ready rms_spread sum_spread")
        scores_done, rms_copied, score_ready, nmax_ready, exp_ready, rsum_ready = sems(
            "scores_done rms_copied score_ready nmax_ready exp_ready rsum_ready")
        attn_ready, attn_hi_ready, attn_split = sems("attn_ready attn_hi_ready attn_split")
        r_done, z_done, hn_done, xn_done, r_act, z_act, hn_act = sems(
            "r_done z_done hn_done xn_done r_act z_act hn_act")
        n_act = sem("n_act")
        rn_ready, pre_ready, diff_ready, zd_ready, h_ready, w_hi_ready, w_lo_ready = sems(
            "rn_ready pre_ready diff_ready zd_ready h_ready w_hi_ready w_lo_ready")
        h_turned, x1_ready, xn_hi_ready, xn_lo_ready, logits_done = sems(
            "h_turned x1_ready xn_hi_ready xn_lo_ready logits_done")
        route, gap_arg, gap_ready, cw_chain, cw_split, cw_turned, cwrow_ready = sems(
            "route gap_arg gap_ready cw_chain cw_split cw_turned cwrow_ready")
        up_done, cw_spread, gelu_done, scaled, g_hi_ready, v_lo_ready, g_lo_ready = sems(
            "up_done cw_spread gelu_done scaled g_hi_ready v_lo_ready g_lo_ready")
        down_done = sem("down_done")
        y_copied, y_turned, y_added = sems("y_copied y_turned y_added")

        block = ctx.enter_context(nc.Block())

        x_v = x.rearrange("b (j p) d -> p (b j) d", p=P)
        out_v = out.rearrange("b (j p) d -> b p j d", p=P)

        @block.sync
        def _(sp):
            sp.dma_start(x_tok[:, 0:NT, :], x_v[:, 0:NT, :]).then_inc(in_x[0], 16)
            sp.dma_start(ctx_tok[:], ctx_in.rearrange("b m d -> m b d")).then_inc(in_ctx, 16)
            sp.dma_start(rows[0:3, :], bih.rearrange("(a d) -> a d", d=D)).then_inc(in_rows, 16)
            sp.dma_start(rows[3:6, :], bhh.rearrange("(a d) -> a d", d=D)).then_inc(in_rows, 16)
            sp.dma_start(rows[6:7, :], slot_w.rearrange("(a d) -> a d", a=1)).then_inc(in_rows, 16)
            sp.dma_start(rows[7:8, :], input_w.rearrange("(a d) -> a d", a=1)).then_inc(in_rows, 16)
            for b in range(1, B):
                sp.dma_start(x_tok[:, b * NT:(b + 1) * NT, :], x_v[:, b * NT:(b + 1) * NT, :]).then_inc(in_x[b], 16)
            sp.dma_start(w_up[:, 0:FH, :], W1.rearrange("d (h f) -> d h f", f=P)).then_inc(in_ffn, 16)
            sp.dma_start(w_ffn[:, FH * P:NF * P].rearrange("d (e f) -> d e f", e=E),
                         Wu.rearrange("e d f -> d e f")).then_inc(in_ffn, 16)
            sp.dma_start(w_down[:, 0:FH, :], W2.rearrange("(h f) d -> f h d", f=P)).then_inc(in_ffn, 16)
            sp.dma_start(w_down[:, FH:NF, :], Wd.rearrange("e (h f) d -> f (e h) d", f=P)).then_inc(in_ffn, 16)
            sp.dma_start(wg_sb[:], Wg).then_inc(in_wg, 16)
            for c in range(B):
                sp.wait_ge(y_added, c + 1)
                sp.dma_start(out_v[c], y_out[:, c * NT:(c + 1) * NT, :]).then_inc(out_stored, 16)
            sp.wait_ge(out_stored, 16 * B)

        @block.gpsimd
        def _(pool):
            nc.gpsimd.memset(ident[:], 0.0).then_inc(ident_zeroed, 1)
            pool.wait_ge(ident_zeroed, 1)
            nc.gpsimd.affine_select(out=ident[:], in_=ident[:], compare_op=ALU.not_equal, fill=1.0, base=0,
                                    pattern=[[-1, P]], channel_multiplier=1).then_inc(ident_ready, 1)
            nc.gpsimd.memset(earlier[:], 1.0).then_inc(mask_set, 1)
            pool.wait_ge(mask_set, 1)
            nc.gpsimd.affine_select(out=earlier[:], in_=earlier[:], compare_op=ALU.is_gt, fill=0.0, base=0,
                                    pattern=[[1, E], [-1, E]], channel_multiplier=0).then_inc(mask_ready, 1)
            nc.gpsimd.memset(vals_hi[:].bitcast(fp32), 0.0).then_inc(pads_zeroed, 1)
            nc.gpsimd.memset(attn_hi.bitcast(fp32), 0.0).then_inc(pads_zeroed, 1)
            pool.wait_ge(powers_ready, 1)

            def variance_to_rstd(n, slot):
                pool.wait_ge(ln_var, n + 1)
                nc.gpsimd.tensor_tensor(ln_r[:, slot, :], var_e[:, slot, :], powers[:], ALU.pow).then_inc(ln_rstd, 1)

            def low_half(s, b):
                pool.wait_ge(hi_ready, s + 1)
                nc.gpsimd.tensor_tensor(in_lo[:, b * S:(b + 1) * S], h_t[:, b, :],
                                        in_hi[:, b * S:(b + 1) * S].bitcast(fp32), ALU.subtract).then_inc(lo_ready, 1)

            def body(k, b, lo):
                on = lambda first, last: lo is None or first <= lo <= last
                if on(-2, STEPS - 3):
                    pool.wait_ge(rms_arg, k + 3)
                    nc.gpsimd.tensor_tensor(fac[:, 0:NT], stat[:, 0:NT], powers[:], ALU.pow).then_inc(rms_ready, 1)
                if on(-1, STEPS - 3):
                    if on(1, LAST):
                        pool.wait_ge(w_hi_ready, k)
                    low_half(k + 2, (b + 2) % B)
                if on(1, LAST):
                    part = bass.ds((k - 1) * WPART, WPART)
                    nc.gpsimd.tensor_tensor(w_lo[:, part], w_ffn[:, part], w_hi[:, part].bitcast(fp32),
                                            ALU.subtract).then_inc(w_lo_ready, 1)

            variance_to_rstd(0, 0)
            variance_to_rstd(1, 1)
            body(-2, (-2) % B, -2)
            low_half(0, 0)
            pool.wait_ge(ctx_mean, 1)
            nc.gpsimd.tensor_tensor(ctx_rms[:], ctx_ms[:], powers[0:M, 0:B], ALU.pow).then_inc(ctx_rstd, 1)
            nc.gpsimd.memset(vals_lo[:].bitcast(fp32), 0.0).then_inc(pads_zeroed, 1)
            variance_to_rstd(2, 0)
            body(-1, (-1) % B, -1)
            nc.gpsimd.memset(attn_lo.bitcast(fp32), 0.0).then_inc(pads_zeroed, 1)
            variance_to_rstd(3, 1)
            body(0, 0, 0)
            with pool.Fori(1, LAST - B + 2, B) as i:
                for j in range(B):
                    body(i + j, (1 + j) % B, None)
            for k in range(LAST + 1, STEPS - 1):
                body(k, k % B, k)
            variance_to_rstd(B, 0)

            def difference(s):
                pool.wait_ge(n_act, s + 1)
                pool.wait_ge(zd_ready, s)
                b = s % B
                nc.gpsimd.tensor_tensor(diff[:], h_t[:, b, :], nn[:, b % 2, :], ALU.subtract).then_inc(diff_ready, 1)

            difference(STEPS - 2)

            def chunk(c, static):
                for f in GLOW:
                    if f == 8 and static == 0:
                        difference(STEPS - 1)
                    if f == 5 and static != B - 1:
                        variance_to_rstd(B + c + 1, 0)
                    pool.wait_ge(g_hi_ready, NF * c + f + 1)
                    nc.gpsimd.tensor_tensor(g_lo[:, f % HLR, :], gc[:, f % GR, :], g_hi[:, f % HLR, :].bitcast(fp32),
                                            ALU.subtract).then_inc(g_lo_ready, 1)

            chunk(0, 0)
            with pool.Fori(1, B - 1) as c:
                chunk(c, None)
            chunk(B - 1, B - 1)

        @block.scalar
        def _(act):
            act.dma_start(wk_nat[:], Wk).then_inc(in_wkq, 16)
            act.dma_start(wq_nat[:], Wq).then_inc(in_wkq, 16)
            act.dma_start(gru_nat[:, 0:3, :], Wih.rearrange("(a p) d -> p a d", p=P)).then_inc(in_gru[0], 16)
            act.dma_start(wv_nat[:], Wv).then_inc(in_wv, 16)
            act.dma_start(gru_nat[:, 3:6, :], Whh.rearrange("(a p) d -> p a d", p=P)).then_inc(in_gru[1], 16)
            act.wait_ge(ones_ready, 1)
            nc.scalar.activation(warm[:], ones[:], ACT.Exp)
            act.wait_ge(ctx_turned, 1)
            nc.scalar.activation(ctx_t[:], bank[3][:, 0:B * M], ACT.Copy).then_inc(ctx_copied, 1)

            def first_slots(b):
                act.wait_ge(ln_turned, b + 1)
                nc.scalar.activation(h_t[:, b, :], bank[6 + b % 2][:], ACT.Copy).then_inc(ln_copied, 1)

            def square(s, b, lo):
                if lo is None or lo >= B:
                    act.wait_ge(h_ready, s - B + 1)
                else:
                    act.wait_ge(ln_copied, s + 1)
                nc.scalar.activation(sq[:, b % 2, :], h_t[:, b, :], ACT.Square).then_inc(sq_ready, 1)

            def high_half(b):
                nc.scalar.activation(in_hi[:, b * S:(b + 1) * S], h_t[:, b, :], ACT.Copy).then_inc(hi_ready, 1)

            def vals_high(b):
                act.wait_ge(vals_done, b + 1)
                nc.scalar.activation(vals_hi[0:M, b, :], VALS[b][0:M, 0:GATES], ACT.Copy,
                                     scale=ctx_rms[:, b:b + 1]).then_inc(vals_hi_ready, 1)

            def candidate(s, p):
                act.wait_ge(pre_ready, s + 1)
                nc.scalar.activation(nn[:, p, :], pre[:], ACT.Tanh, bias=cols[:, 2:3]).then_inc(n_act, 1)

            def body(k, b, lo, fill=lambda: None):
                on = lambda first, last: lo is None or first <= lo <= last
                if on(0, STEPS - 1):
                    act.wait_ge(attn_ready, k + 1)
                    nc.scalar.activation(attn_hi[0:M, b % 2, :], attn[:], ACT.Copy).then_inc(attn_hi_ready, 1)
                if on(-1, STEPS - 2):
                    p = (b + 1) % 2
                    act.wait_ge(nmax_ready, k + 2)
                    nc.scalar.activation(expo[:, p, :], score[:, p, :], ACT.Exp, bias=nmax[:, p:p + 1],
                                         scale=ctx_rms[:, (b + 1) % B:(b + 1) % B + 1],
                                         accum_out=esum[:, p:p + 1]).then_inc(exp_ready, 1)
                if on(-2, STEPS - 3):
                    high_half((b + 2) % B)
                fill()
                if on(1, STEPS - 1):
                    candidate(k - 1, (b - 1) % 2)
                if on(0, STEPS - 1):
                    if on(1, STEPS - 1):
                        act.wait_ge(rn_ready, k)
                    act.wait_ge(hn_done, k + 1)
                    nc.scalar.activation(hn[:], HNB[:], ACT.Identity, scale=0.5, bias=half_b[:, 2:3]).then_inc(hn_act, 1)
                    act.wait_ge(r_done, k + 1)
                    nc.scalar.activation(tr[:], RB[:], ACT.Tanh, scale=0.5, bias=half_b[:, 0:1]).then_inc(r_act, 1)
                    if lo == STEPS - 1:
                        act.wait_ge(zd_ready, k - 1)
                    act.wait_ge(z_done, k + 1)
                    nc.scalar.activation(tz[:, b % 2, :], ZB[:], ACT.Tanh, scale=0.5, bias=half_b[:, 1:2]).then_inc(z_act, 1)
                if on(-2, STEPS - 3):
                    act.wait_ge(rms_spread, k + 3)
                    nc.scalar.activation(rms_b[:], RMSB[0:M, :], ACT.Copy).then_inc(rms_copied, 1)
                if on(0, STEPS - 4):
                    square(k + 3, (b + 3) % B, None if lo is None else lo + 3)

            def context_sums():
                act.wait_ge(in_ctx, 16)
                for b in range(B):
                    nc.scalar.activation(ctx_sq[:, b * D:(b + 1) * D], ctx_tok[:, b, :], ACT.Square,
                                         accum_out=ctx_ss[:, b:b + 1]).then_inc(ctx_squared, 1)

            def first_values():
                act.wait_ge(pads_zeroed, 1)
                vals_high(0)
                vals_high(1)
                vals_high(2)
                first_slots(2)
                square(2, 2, 2)

            act.wait_ge(keyw_done, 1)
            act.wait_ge(cols_copied, 1)
            nc.scalar.activation(key_w[:], bank[1][:, 0:D], ACT.Copy, scale=cols[:, 7:8]).then_inc(keyw_ready, 1)
            first_slots(0)
            square(0, 0, 0)
            body(-2, (-2) % B, -2, context_sums)
            act.wait_ge(gru_turned, 1)
            nc.scalar.activation(wih_t[:], bank[4][:, 0:GATES], ACT.Copy).then_inc(wih_ready, 1)
            first_slots(1)
            square(1, 1, 1)
            act.wait_ge(gru_turned, 2)
            nc.scalar.activation(whh_hi[:], bank[5][:, 0:GATES], ACT.Copy).then_inc(whh_hi_ready, 1)
            act.wait_ge(valw_done, 1)
            nc.scalar.activation(val_w[:], bank[3][:, 0:GATES], ACT.Copy, scale=cols[:, 7:8]).then_inc(valw_ready, 1)
            act.wait_ge(ctx_rstd, 1)
            body(-1, (-1) % B, -1, first_values)
            vals_high(3)
            act.wait_ge(pads_zeroed, 2)
            act.wait_ge(bias_ready, 1)
            body(0, 0, 0, lambda: first_slots(3))
            with act.Fori(1, LAST - B + 2, B) as i:
                for j in range(B):
                    body(i + j, (1 + j) % B, None)
            def expert_input(b):
                act.wait_ge(ln_turned, B + b + 1)
                nc.scalar.activation(xn_t[:], MID[:], ACT.Copy).then_inc(ln_copied, 1)
                nc.scalar.activation(in_hi[:, bass.ds(b * S, S)], MID[:], ACT.Copy).then_inc(xn_hi_ready, 1)

            def load_table():
                nc.scalar.activation(warm[:], ones[:], ACT.Gelu)

            for k in range(LAST + 1, STEPS - 2):
                body(k, k % B, k)
            body(STEPS - 2, (STEPS - 2) % B, STEPS - 2, load_table)
            body(STEPS - 1, (STEPS - 1) % B, STEPS - 1, lambda: expert_input(0))

            def gap(b):
                act.wait_ge(gap_arg, b + 1)
                nc.scalar.activation(tgap[:], arg[:], ACT.Tanh).then_inc(gap_ready, 1)

            def weight_rows(b):
                nc.scalar.activation(cw_row[:, bass.ds(b * S, S)], MID[0:2 * E, :], ACT.Copy).then_inc(cwrow_ready, 1)

            def hidden_high(c, f, wrapped):
                if f >= FH:
                    act.wait_ge(scaled, NX * c + f - FH + 1)
                if f >= HLR or wrapped:
                    act.wait_ge(down_done, NF * c + f - HLR + 1)
                if f == 0 and not wrapped:
                    act.wait_ge(xn_done, STEPS)
                src = gc if f >= FH else g
                nc.scalar.activation(g_hi[:, f % HLR, :], src[:, f % GR, :], ACT.Copy).then_inc(g_hi_ready, 1)

            def copy_y(c):
                act.wait_ge(down_done, NF * (c + 1))
                nc.scalar.activation(y_t, Y[:], ACT.Copy).then_inc(y_copied, 1)

            def chunk(c, static):
                for f in range(NF):
                    if f == 2 and static == 0:
                        gap(0)
                    if f == 3 and static == 0:
                        act.wait_ge(cw_turned, 1)
                        weight_rows(0)
                        candidate(STEPS - 1, (STEPS - 1) % 2)
                    if f == LAG and static != 0:
                        copy_y(c - 1)
                    if f == 9 and static != B - 1:
                        expert_input(c + 1)
                    if f == 15 and static != B - 1:
                        gap(c + 1)
                    if GR <= f < GR + FH:
                        act.wait_ge(v_lo_ready, len(VLOW) * c + f - GR + 1)
                    if f == 17 and static != B - 1:
                        act.wait_ge(cw_turned, c + 2)
                    act.wait_ge(up_done, NF * c + f + 1)
                    nc.scalar.activation(g[:, f % GR, :], UP[f % UPR][:], ACT.Gelu).then_inc(gelu_done, 1)
                    if f:
                        if f == 1 or f == 2:
                            act.wait_ge(gelu_done, NF * c + f)
                        hidden_high(c, f - 1, static != 0)
                    if f == 17 and static != B - 1:
                        weight_rows(c + 1)
                hidden_high(c, NF - 1, static != 0)

            chunk(0, 0)
            with act.Fori(1, B - 1) as c:
                chunk(c, None)
            chunk(B - 1, B - 1)
            copy_y(B - 1)

        @block.vector
        def _(dve):
            nc.vector.memset(w_hi[:, 0:S].bitcast(fp32), 0.0).then_inc(idle_ready, 1)
            nc.vector.memset(ones[:], 1.0).then_inc(ones_ready, 1)
            nc.vector.memset(powers[:], -0.5).then_inc(powers_ready, 1)
            nc.vector.memset(fac[:, NT:NQ], 1.0).then_inc(fac_set, 1)
            dve.wait_ge(ident_ready, 1)
            nc.vector.tensor_tensor(sel_sum[:], ident[0:2 * NQ, 0:NQ], ident[0:2 * NQ, NQ:2 * NQ],
                                    ALU.add).then_inc(selsum_ready, 1)
            dve.wait_ge(selsum_ready, 1)
            nc.vector.tensor_copy(sel[:], sel_sum[:].unsqueeze(2).broadcast_to([2 * NQ, NQ, P])).then_inc(sel_ready, 1)

            def rows_at(b, j):
                return x_tok[:, bass.ds(b * NT + j, 1), :].rearrange("p o d -> p (o d)")

            def row_stats(slot, b):
                for j in range(NT):
                    nc.vector.bn_stats(bn[:, slot, j, :], rows_at(b, j)).then_inc(ln_stats, 1)

            def row_moments(slot):
                for j in range(NT):
                    nc.vector.bn_aggr(mv[:, slot, j, :], bn[:, slot, j, :]).then_inc(ln_mv, 1)

            def variance_plus_eps(n, slot):
                dve.wait_ge(ln_mv, NT * (n + 1))
                nc.vector.tensor_scalar(var_e[:, slot, :], mv[:, slot, :, 1], LN_EPS, None, ALU.add).then_inc(ln_var, 1)

            def layer_norm_factors(n, slot, b):
                row_stats(slot, b)
                dve.wait_ge(ln_stats, NT * (n + 1))
                row_moments(slot)
                variance_plus_eps(n, slot)

            def normalise(n, slot, b, turned):
                dve.wait_ge(ln_rstd, n + 1)
                if turned is not None:
                    dve.wait_ge(ln_turned, turned)
                for j in range(NT):
                    last = nc.vector.tensor_scalar(xn_tok[:, slot, j, :], rows_at(b, j), mv[:, slot, j, 0:1],
                                                   ln_r[:, slot, j:j + 1], ALU.subtract, ALU.mult)
                last.then_inc(ln_scaled, 1)

            dve.wait_ge(in_x[0], 16)
            layer_norm_factors(0, 0, 0)
            normalise(0, 0, 0, None)
            dve.wait_ge(cols_done, 1)
            nc.vector.tensor_copy(cols[:], bank[2][:, 0:8]).then_inc(cols_copied, 1)
            dve.wait_ge(in_x[1], 16)
            layer_norm_factors(1, 1, 1)

            def split_keys():
                dve.wait_ge(keys_done, 1)
                nc.vector.tensor_scalar(keys[:], bank[5][:, 0:B * M], cols[:, 6:7], SCALE,
                                        ALU.mult, ALU.mult).then_inc(keys_copied, 1)
                dve.wait_ge(keys_copied, 1)
                nc.vector.tensor_copy(keys_hi[:], keys[:]).then_inc(keys_hi_ready, 1)
                dve.wait_ge(keys_hi_ready, 1)
                nc.vector.tensor_tensor(keys_lo[:], keys[:], keys_hi[:].bitcast(fp32), ALU.subtract).then_inc(keys_ready, 1)

            def vals_low(b):
                if b == 0:
                    dve.wait_ge(pads_zeroed, 3)
                dve.wait_ge(vals_hi_ready, b + 1)
                nc.vector.scalar_tensor_tensor(vals_lo[0:M, b, :], VALS[b][0:M, 0:GATES], ctx_rms[:, b:b + 1],
                                               vals_hi[0:M, b, :].bitcast(fp32), ALU.mult, ALU.subtract).then_inc(vals_ready, 1)

            def reset(s):
                dve.wait_ge(r_act, s + 1)
                dve.wait_ge(hn_act, s + 1)
                nc.vector.scalar_tensor_tensor(rn[:], tr[:], 1.0, hn[:], ALU.add, ALU.mult).then_inc(rn_ready, 1)

            def argument(s):
                dve.wait_ge(xn_done, s + 1)
                dve.wait_ge(rn_ready, s + 1)
                nc.vector.tensor_tensor(pre[:], rn[:], XNB[:], ALU.add).then_inc(pre_ready, 1)

            def difference(s, b):
                dve.wait_ge(n_act, s + 1)
                nc.vector.tensor_tensor(diff[:], h_t[:, b, :], nn[:, b % 2, :], ALU.subtract).then_inc(diff_ready, 1)

            def scaled_difference(s, b):
                dve.wait_ge(diff_ready, s + 1)
                nc.vector.scalar_tensor_tensor(zd[:], tz[:, b % 2, :], 1.0, diff[:], ALU.add, ALU.mult).then_inc(zd_ready, 1)

            def new_slots(s, b):
                dve.wait_ge(zd_ready, s + 1)
                nc.vector.scalar_tensor_tensor(h_t[:, b, :], zd[:], 0.5, nn[:, b % 2, :],
                                               ALU.mult, ALU.add).then_inc(h_ready, 1)

            def weights_low(s, p, first):
                dve.wait_ge(attn_hi_ready, s + 1)
                if first:
                    dve.wait_ge(pads_zeroed, 4)
                nc.vector.tensor_tensor(attn_lo[0:M, p, :], attn[:], attn_hi[0:M, p, :].bitcast(fp32),
                                        ALU.subtract).then_inc(attn_split, 1)

            def weights(s, p):
                nc.vector.scalar_tensor_tensor(attn[:], expo[:, p, :], rsum[:, p:p + 1], SUMB[0:M, :],
                                               ALU.mult, ALU.mult).then_inc(attn_ready, 1)

            def first_norm_variances():
                dve.wait_ge(ln_stats, NT * (B + 1))
                row_moments(0)
                variance_plus_eps(B, 0)

            def body(k, b, lo, fills=()):
                on = lambda first, last: lo is None or first <= lo <= last
                fill = lambda i: fills[i]() if i < len(fills) and fills[i] else None
                if on(0, STEPS - 1):
                    dve.wait_ge(sum_spread, k + 1)
                    if on(0, STEPS - 2):
                        dve.wait_ge(scores_done, k + 2)
                        dve.wait_ge(rms_copied, k + 2)
                    weights(k, b % 2)
                if lo == -1:
                    dve.wait_ge(scores_done, 1)
                    dve.wait_ge(rms_copied, 1)
                if on(-1, STEPS - 2):
                    p = (b + 1) % 2
                    nxt = (b + 1) % B
                    nc.vector.tensor_tensor_reduce(out=score[:, p, :], in0=SCORE[0:M, :], in1=rms_b[:], scale=1.0,
                                                   scalar=-3.0e38, op0=ALU.mult, op1=ALU.max,
                                                   accum_out=smax[:, p:p + 1]).then_inc(score_ready, 1)
                    if lo == -1:
                        dve.wait_ge(ctx_rstd, 1)
                    dve.wait_ge(score_ready, k + 2)
                    nc.vector.tensor_scalar(nmax[:, p:p + 1], smax[:, p:p + 1], ctx_rms[:, nxt:nxt + 1], -1.0,
                                            ALU.mult, ALU.mult).then_inc(nmax_ready, 1)
                if on(1, STEPS - 2):
                    reset(k - 1)
                fill(0)
                if on(-2, STEPS - 3):
                    dve.wait_ge(sq_summed, k + 3)
                    nc.vector.tensor_scalar(stat[:, 0:NT], SMALL[:, 0:NT], 1.0 / D, RMS_EPS,
                                            ALU.mult, ALU.add).then_inc(rms_arg, 1)
                if on(1, LAST):
                    if lo is None or lo == 1:
                        dve.wait_ge(in_ffn, 64)
                    part = bass.ds((k - 1) * WPART, WPART)
                    nc.vector.tensor_scalar(w_hi[:, part], w_ffn[:, part], 1.0, None, ALU.mult).then_inc(w_hi_ready, 1)
                if on(-1, STEPS - 2):
                    p = (b + 1) % 2
                    dve.wait_ge(exp_ready, k + 2)
                    nc.vector.reciprocal(rsum[:, p:p + 1], esum[:, p:p + 1]).then_inc(rsum_ready, 1)
                if on(0, STEPS - 1):
                    weights_low(k, b % 2, lo == 0)
                if lo == STEPS - 1:
                    reset(k - 1)
                if on(1, STEPS - 1):
                    argument(k - 1)
                fill(1)
                if on(-1, STEPS - 2):
                    dve.wait_ge(attn_summed, k + 2)
                    nc.vector.tensor_scalar(stat[:, NT:NQ], SMALL[:, NT:NQ], SUM_EPS, None, ALU.add).then_inc(sum_arg, 1)
                    dve.wait_ge(sum_arg, k + 2)
                    nc.vector.reciprocal(fac[:, NT:NQ], stat[:, NT:NQ]).then_inc(sum_ready, 1)
                if on(-2, STEPS - 2):
                    if on(-2, STEPS - 3):
                        dve.wait_ge(rms_ready, k + 3)
                    if on(-1, STEPS - 2):
                        dve.wait_ge(sum_ready, k + 2)
                    else:
                        dve.wait_ge(fac_set, 1)
                    nc.vector.tensor_copy(fac_hl[:, 0:NQ], fac[:]).then_inc(fac_hi, 1)
                    dve.wait_ge(fac_hi, k + 3)
                    nc.vector.tensor_tensor(fac_hl[:, NQ:2 * NQ], fac[:], fac_hl[:, 0:NQ].bitcast(fp32),
                                            ALU.subtract).then_inc(fac_split, 1)
                if lo == STEPS - 2:
                    first_norm_variances()
                elif on(1, STEPS - 3):
                    difference(k - 1, (b - 1) % B)
                if on(-2, STEPS - 2):
                    dve.wait_ge(fac_turned, k + 3)
                    nc.vector.tensor_copy(fac_row[:], SMALL[0:2 * NQ, P:2 * P]).then_inc(row_ready, 1)
                if lo == STEPS - 2:
                    difference(k - 1, (b - 1) % B)
                elif on(1, STEPS - 3):
                    scaled_difference(k - 1, (b - 1) % B)
                    new_slots(k - 1, (b - 1) % B)
                fill(2)

            body(-2, (-2) % B, -2, (None, split_keys))
            dve.wait_ge(ctx_squared, B)
            nc.vector.tensor_scalar(ctx_ms[:], ctx_ss[:], 1.0 / D, RMS_EPS, ALU.mult, ALU.add).then_inc(ctx_mean, 1)
            normalise(1, 1, 1, None)
            dve.wait_ge(in_x[2], 16)
            layer_norm_factors(2, 0, 2)

            def second_norm():
                dve.wait_ge(whh_hi_ready, 1)
                nc.vector.tensor_tensor(whh_lo[:], bank[5][:, 0:GATES], whh_hi[:].bitcast(fp32),
                                        ALU.subtract).then_inc(whh_ready, 1)
                normalise(2, 0, 2, 1)

            def first_values():
                nc.vector.tensor_tensor(half_b[:, 0:2], cols[:, 0:2], cols[:, 3:5], ALU.add).then_inc(bias_sum, 1)
                nc.vector.tensor_copy(half_b[:, 2:3], cols[:, 5:6]).then_inc(bias_sum, 1)
                dve.wait_ge(in_x[3], 16)
                row_stats(1, 3)
                vals_low(0)
                dve.wait_ge(bias_sum, 2)
                nc.vector.tensor_scalar(half_b[:], half_b[:], 0.5, None, ALU.mult).then_inc(bias_ready, 1)

            def last_norm():
                vals_low(3)
                normalise(3, 1, 3, 2)

            body(-1, (-1) % B, -1, (second_norm, first_values))
            dve.wait_ge(ln_stats, NT * B)
            row_moments(1)
            vals_low(1)
            variance_plus_eps(3, 1)
            vals_low(2)
            body(0, 0, 0, (last_norm,))
            with dve.Fori(1, LAST - B + 2, B) as i:
                for j in range(B):
                    body(i + j, (1 + j) % B, None)

            def residual(b, turned=T):
                dve.wait_ge(h_turned, b + 1)
                nc.vector.tensor_tensor(x_tok[:, b * NT:(b + 1) * NT, :], x_tok[:, b * NT:(b + 1) * NT, :],
                                        turned[:].rearrange("p (j d) -> p j d", d=D), ALU.add).then_inc(x1_ready, 1)

            def input_low(b):
                dve.wait_ge(xn_hi_ready, b + 1)
                own = bass.ds(b * S, S)
                nc.vector.tensor_tensor(in_lo[:, own], xn_t[:], in_hi[:, own].bitcast(fp32),
                                        ALU.subtract).then_inc(xn_lo_ready, 1)

            def compare_logits(b):
                own = lg[:].unsqueeze(3).broadcast_to([P, NT, E, E])
                other = lg[:].unsqueeze(2).broadcast_to([P, NT, E, E])
                dve.wait_ge(logits_done, b + 1)
                nc.vector.tensor_copy(lg[:], T[:, 0:NT * E].rearrange("p (j e) -> p j e", e=E)).then_inc(route, 1)
                dve.wait_ge(route, ROUTE * b + 1)
                nc.vector.tensor_tensor(eq[:], other, own, ALU.is_equal).then_inc(route, 1)
                nc.vector.tensor_tensor(gt[:], other, own, ALU.is_gt).then_inc(route, 1)

            def break_ties(b):
                flat = lambda t: t[:].rearrange("p j e f -> p j (e f)")
                dve.wait_ge(route, ROUTE * b + 2)
                nc.vector.tensor_tensor(flat(tie), flat(eq), earlier[:].rearrange("p e f -> p (e f)").unsqueeze(1)
                                        .broadcast_to([P, NT, E * E]), ALU.mult).then_inc(route, 1)
                dve.wait_ge(route, ROUTE * b + 4)
                nc.vector.tensor_tensor(flat(ahead), flat(tie), flat(gt), ALU.add).then_inc(route, 1)

            def take_two(b):
                dve.wait_ge(route, ROUTE * b + 5)
                nc.vector.reduce_sum(rank[:], ahead[:], AX.X).then_inc(route, 1)
                dve.wait_ge(route, ROUTE * b + 6)
                nc.vector.scalar_tensor_tensor(top[:], rank[:], 1.5, lg[:], ALU.is_lt, ALU.mult).then_inc(route, 1)
                nc.vector.tensor_scalar(half_top[:], rank[:], 1.5, 0.5, ALU.is_lt, ALU.mult).then_inc(route, 1)
                dve.wait_ge(route, ROUTE * b + 7)
                nc.vector.reduce_sum(pair[:], top[:], AX.X).then_inc(route, 1)
                dve.wait_ge(route, ROUTE * b + 9)
                nc.vector.scalar_tensor_tensor(arg[:], pair[:].unsqueeze(2).broadcast_to([P, NT, E]), -0.5, lg[:],
                                               ALU.mult, ALU.add).then_inc(gap_arg, 1)

            def weigh_experts(b, first):
                dve.wait_ge(gap_ready, b + 1)
                nc.vector.scalar_tensor_tensor(cw[:], tgap[:], 1.0, half_top[:], ALU.add, ALU.mult).then_inc(cw_chain, 1)
                dve.wait_ge(cw_chain, 2 * b + 1)
                if not first:
                    dve.wait_ge(cw_turned, b)
                nc.vector.tensor_copy(cw_hl[:, :, 0, :], cw[:]).then_inc(cw_chain, 1)
                dve.wait_ge(cw_chain, 2 * b + 2)
                nc.vector.tensor_tensor(cw_hl[:, :, 1, :], cw[:], cw_hl[:, :, 0, :].bitcast(fp32),
                                        ALU.subtract).then_inc(cw_split, 1)

            def first_norm_stats():
                dve.wait_ge(x1_ready, 1)
                row_stats(0, 0)

            for k in range(LAST + 1, STEPS - 2):
                body(k, k % B, k)
            body(STEPS - 2, (STEPS - 2) % B, STEPS - 2, (lambda: residual(0, MID), first_norm_stats))
            body(STEPS - 1, (STEPS - 1) % B, STEPS - 1, (lambda: normalise(B, 0, 0, 3),))
            input_low(0)
            scaled_difference(STEPS - 3, (STEPS - 3) % B)
            dve.wait_ge(mask_ready, 1)
            compare_logits(0)
            break_ties(0)
            take_two(0)
            reset(STEPS - 1)
            weigh_experts(0, True)
            new_slots(STEPS - 3, (STEPS - 3) % B)
            argument(STEPS - 1)

            def store(c):
                dve.wait_ge(y_turned, c + 1)
                own = bass.ds(c * NT, NT)
                nc.vector.tensor_tensor(y_out[:, own, :], x_tok[:, own, :], T[:].rearrange("p (j d) -> p j d", d=D),
                                        ALU.add).then_inc(y_added, 1)

            def low_half(c, f):
                dve.wait_ge(g_hi_ready, NF * c + f + 1)
                src = gc if f >= FH else g
                nc.vector.tensor_tensor(g_lo[:, f % HLR, :], src[:, f % GR, :], g_hi[:, f % HLR, :].bitcast(fp32),
                                        ALU.subtract).then_inc(v_lo_ready, 1)

            def between(c, f, static):
                last, prepare = STEPS - 1, static != B - 1
                if static == 0:
                    if f == 2:
                        residual(1)
                    if f == 5:
                        scaled_difference(last - 1, (last - 1) % B)
                    if f == 8:
                        new_slots(last - 1, (last - 1) % B)
                    if f == 10:
                        scaled_difference(last, last % B)
                    if f == 14:
                        residual(2)
                    if f == 16:
                        new_slots(last, last % B)
                    if f == 17:
                        residual(3)
                elif f == 5:
                    store(c - 1)
                if not prepare:
                    return
                if f == 3 or (f == 0 and static != 0):
                    if static == 0:
                        dve.wait_ge(x1_ready, 2)
                        tiles = range(NT)
                    elif f == 0:
                        dve.wait_ge(x1_ready, B)
                        tiles = range(NT // 2)
                    else:
                        tiles = range(NT // 2, NT)
                    for j in tiles:
                        nc.vector.bn_stats(bn[:, 0, j, :], rows_at(c + 1, j)).then_inc(ln_stats, 1)
                if f == 4:
                    row_moments(0)
                    variance_plus_eps(B + c + 1, 0)
                if f == 6:
                    normalise(B + c + 1, 0, c + 1, B + c + 1)
                if f == 9:
                    input_low(c + 1)
                if f == 11:
                    compare_logits(c + 1)
                if f == 12:
                    break_ties(c + 1)
                if f == 13:
                    take_two(c + 1)
                if f == 15:
                    weigh_experts(c + 1, False)

            def chunk(c, static):
                for f in range(NF):
                    if f >= FH:
                        e = (f - FH) // FH
                        if f == 4 and static != B - 1:
                            dve.wait_ge(ln_stats, NT * (B + c + 2))
                        if f % FH == 0:
                            dve.wait_ge(cw_spread, E * c + e + 1)
                        if f < FH + GR:
                            if static != 0:
                                prior = NF - GR + f % GR
                                if prior in VLOW:
                                    dve.wait_ge(v_lo_ready, len(VLOW) * (c - 1) + VLOW.index(prior) + 1)
                                else:
                                    dve.wait_ge(g_lo_ready, len(GLOW) * (c - 1) + GLOW.index(prior) + 1)
                        elif f - GR in VLOW:
                            dve.wait_ge(v_lo_ready, len(VLOW) * c + VLOW.index(f - GR) + 1)
                        else:
                            dve.wait_ge(g_lo_ready, len(GLOW) * c + GLOW.index(f - GR) + 1)
                        dve.wait_ge(gelu_done, NF * c + f + 1)
                        nc.vector.tensor_tensor(gc[:, f % GR, :], g[:, f % GR, :], CB[e % 2][:],
                                                ALU.mult).then_inc(scaled, 1)
                    if f - 1 in VLOW:
                        low_half(c, f - 1)
                    between(c, f, static)
                low_half(c, NF - 1)

            chunk(0, 0)
            with dve.Fori(1, B - 1) as c:
                chunk(c, None)
            chunk(B - 1, B - 1)
            store(B - 1)

        @block.tensor
        def _(pe):
            def split_mm(dst, w_h, w_l, a_h, a_l, start=True, stop=True):
                nc.tensor.matmul(dst, w_h, a_l, start=start, stop=False)
                nc.tensor.matmul(dst, w_l, a_h, start=False, stop=False)
                return nc.tensor.matmul(dst, w_h, a_h, start=False, stop=stop)

            def idle(dst, n):
                for _ in range(n):
                    nc.tensor.matmul(dst[:], w_hi[:, 0:P], w_hi[:, 0:S], start=True, stop=True)

            pe.wait_ge(idle_ready, 1)
            idle(bank[7], 8)
            pe.wait_ge(ident_ready, 1)
            pe.wait_ge(in_ctx, 16)
            for b in range(B):
                last = nc.tensor.transpose(bank[3][:, b * M:(b + 1) * M], ctx_tok[:, b, :], ident[0:M, 0:M])
            last.then_inc(ctx_turned, 1)
            pe.wait_ge(in_wkq, 32)
            nc.tensor.matmul(bank[1][:, 0:D], wk_nat[:], wq_nat[:], start=True, stop=True).then_inc(keyw_done, 1)
            idle(bank[7], 3)

            def turn_gru(n):
                pe.wait_ge(in_gru[n], 16)
                if n == 1:
                    pe.wait_ge(keys_copied, 1)
                for a in range(3):
                    last = nc.tensor.transpose(bank[4 + n][:, a * P:(a + 1) * P], gru_nat[:, 3 * n + a, :], ident[:])
                last.then_inc(gru_turned, 1)

            def turn_norm(n, slot, dst):
                pe.wait_ge(ln_scaled, n + 1)
                for j in range(NT):
                    last = nc.tensor.transpose(dst[:, j * P:(j + 1) * P], xn_tok[:, slot, j, :], ident[:])
                last.then_inc(ln_turned, 1)

            def project_values(b):
                nc.tensor.matmul(VALS[b][0:M, 0:GATES], ctx_t[:, b * M:(b + 1) * M], val_w[:],
                                 start=True, stop=True).then_inc(vals_done, 1)

            pe.wait_ge(in_rows, 64)
            nc.tensor.transpose(bank[2][:, 0:8], rows[:], ident[0:8, 0:8]).then_inc(cols_done, 1)
            idle(bank[7], 1)
            turn_norm(0, 0, bank[6])
            turn_gru(0)
            pe.wait_ge(ctx_copied, 1)
            pe.wait_ge(keyw_ready, 1)
            nc.tensor.matmul(bank[5][:, 0:B * M], key_w[:], ctx_t[:], start=True, stop=True).then_inc(keys_done, 1)
            idle(bank[7], 4)

            def body(k, b, lo, fills=()):
                on = lambda first, last: lo is None or first <= lo <= last
                fill = lambda i: fills[i]() if i < len(fills) and fills[i] else None

                def hidden(dst, n, b, stop):
                    own = slice(b * S, (b + 1) * S)
                    cols_of = slice(n * D, (n + 1) * D)
                    return split_mm(dst[:], whh_hi[:, cols_of], whh_lo[:, cols_of], in_hi[:, own], in_lo[:, own],
                                    stop=stop)

                def scores(s):
                    n = (b + 2) % B
                    pe.wait_ge(lo_ready, s + 1)
                    split_mm(SCORE[0:M, :], keys_hi[:, n * M:(n + 1) * M], keys_lo[:, n * M:(n + 1) * M],
                             in_hi[:, n * S:(n + 1) * S], in_lo[:, n * S:(n + 1) * S]).then_inc(scores_done, 1)

                def context(dst, n, start):
                    cols_of = slice(n * D, (n + 1) * D)
                    return split_mm(dst[:], vals_hi[:, b, cols_of], vals_lo[:, b, cols_of], attn_hi[:, b % 2, :],
                                    attn_lo[:, b % 2, :], start=start)

                if on(0, STEPS - 1):
                    if on(1, STEPS - 1):
                        pe.wait_ge(z_act, k)
                    hidden(ZB, 1, b, False)
                if on(-2, STEPS - 3):
                    pe.wait_ge(sq_ready, k + 3)
                    for j in range(NT):
                        last = nc.tensor.matmul(SMALL[:, j:j + 1], sq[:, b % 2, j * P:(j + 1) * P], ones[:],
                                                start=True, stop=True)
                    last.then_inc(sq_summed, 1)
                if on(0, STEPS - 1):
                    if on(1, STEPS - 1):
                        pe.wait_ge(hn_act, k)
                    hidden(HNB, 2, b, True).then_inc(hn_done, 1)
                    if lo == 0:
                        pe.wait_ge(vals_ready, B)
                    hidden(RB, 0, b, False)
                fill(0)
                if on(-1, STEPS - 2):
                    p = (b + 1) % 2
                    pe.wait_ge(rsum_ready, k + 2)
                    for j in range(NT):
                        last = nc.tensor.matmul(SMALL[:, NT + j:NT + j + 1], expo[:, p, j * P:(j + 1) * P],
                                                rsum[:, p:p + 1], start=True, stop=True)
                    last.then_inc(attn_summed, 1)
                fill(1)
                if on(0, STEPS - 1):
                    pe.wait_ge(attn_split, k + 1)
                    context(RB, 0, False).then_inc(r_done, 1)
                    context(ZB, 1, False).then_inc(z_done, 1)
                if on(-2, STEPS - 2):
                    pe.wait_ge(fac_split, k + 3)
                    nc.tensor.transpose(SMALL[0:2 * NQ, P:2 * P], fac_hl[:].bitcast(fp32), ident[:]).then_inc(fac_turned, 1)
                fill(2)
                if on(0, STEPS - 3):
                    scores(k + 2)
                if on(-2, STEPS - 2):
                    pe.wait_ge(row_ready, k + 3)
                if on(-2, STEPS - 3):
                    for j in range(NT):
                        last = nc.tensor.matmul(RMSB[:, j * P:(j + 1) * P], sel[:, j, :], fac_row[:],
                                                start=True, stop=True)
                    last.then_inc(rms_spread, 1)
                if lo == -2:
                    pe.wait_ge(keys_ready, 1)
                    scores(0)
                if on(-1, STEPS - 2):
                    for j in range(NT):
                        last = nc.tensor.matmul(SUMB[:, j * P:(j + 1) * P], sel[:, NT + j, :], fac_row[:],
                                                start=True, stop=True)
                    last.then_inc(sum_spread, 1)
                if lo == -1:
                    scores(1)
                if on(0, STEPS - 1):
                    if on(1, STEPS - 1):
                        pe.wait_ge(pre_ready, k)
                    if lo == 0:
                        pe.wait_ge(ln_copied, B)
                    context(XNB, 2, True).then_inc(xn_done, 1)

            pe.wait_ge(ones_ready, 1)
            pe.wait_ge(sel_ready, 1)
            def first_values():
                pe.wait_ge(valw_ready, 1)
                pe.wait_ge(whh_ready, 1)
                for b in range(3):
                    project_values(b)

            def fourth_values():
                pe.wait_ge(vals_ready, 1)
                project_values(3)

            def fourth_slots():
                pe.wait_ge(vals_ready, 3)
                turn_norm(3, 1, bank[7])

            body(-2, (-2) % B, -2, (None, lambda: idle(bank[7], 6)))
            turn_norm(1, 1, bank[7])
            turn_gru(1)
            pe.wait_ge(in_wv, 16)
            pe.wait_ge(wih_ready, 1)
            nc.tensor.matmul(bank[3][:, 0:GATES], wv_nat[:], wih_t[:], start=True, stop=True).then_inc(valw_done, 1)
            idle(bank[4], 4)
            body(-1, (-1) % B, -1, (first_values, lambda: turn_norm(2, 0, bank[6]), fourth_values))
            pe.wait_ge(vals_ready, 2)
            pe.wait_ge(ln_copied, 3)
            body(0, 0, 0, (None, fourth_slots))
            with pe.Fori(1, LAST - B + 2, B) as i:
                for j in range(B):
                    body(i + j, (1 + j) % B, None)

            def turn_h(b, dst=T):
                pe.wait_ge(h_ready, STEPS - B + b + 1)
                if b == 0:
                    pe.wait_ge(rms_copied, STEPS)
                elif b == 1:
                    pe.wait_ge(route, 1)
                elif b == 2:
                    pe.wait_ge(route, ROUTE + 1)
                else:
                    pe.wait_ge(x1_ready, 3)
                for j in range(NT):
                    last = nc.tensor.transpose(dst[:, j * P:(j + 1) * P], h_t[:, b, j * P:(j + 1) * P], ident[:])
                last.then_inc(h_turned, 1)

            def logits(b):
                pe.wait_ge(xn_hi_ready, b + 1)
                for j in range(NT):
                    last = nc.tensor.matmul(T[:, j * E:(j + 1) * E], xn_t[:, j * P:(j + 1) * P], wg_sb[:],
                                            start=True, stop=True)
                last.then_inc(logits_done, 1)

            def turn_weights(b):
                pe.wait_ge(cw_split, b + 1)
                for j in range(NT):
                    last = nc.tensor.transpose(MID[0:2 * E, j * P:(j + 1) * P],
                                               cw_hl[:, j, :, :].rearrange("p a e -> p (a e)").bitcast(fp32), ident[:])
                last.then_inc(cw_turned, 1)

            def up(c, f, first):
                own = bass.ds(c * S, S)
                n = slice(f * P, (f + 1) * P)
                if f == 0:
                    pe.wait_ge(xn_lo_ready, c + 1)
                if f >= FH and f % FH == 0:
                    e = f // FH - 1
                    if e == 0:
                        if not first:
                            pe.wait_ge(cwrow_ready, c + 1)
                            pe.wait_ge(scaled, NX * c)
                    else:
                        if e >= 2 or not first:
                            pe.wait_ge(scaled, NX * c + FH * (e - 1))
                if f >= UPR or not first:
                    pe.wait_ge(gelu_done, NF * c + f - UPR + 1)
                split_mm(UP[f % UPR][:], w_hi[:, n], w_lo[:, n], in_hi[:, own], in_lo[:, own]).then_inc(up_done, 1)
                if f >= FH and f % FH == 0 and not (first and f <= 2 * FH):
                    spread_weights(c, f // FH - 1)

            def spread_weights(c, e):
                nc.tensor.matmul(CB[e % 2][:], sel[:, e, :], cw_row[:, bass.ds(c * S, S)],
                                 start=True, stop=True).then_inc(cw_spread, 1)

            def down(c, f, static):
                if f in VLOW:
                    pe.wait_ge(v_lo_ready, len(VLOW) * c + VLOW.index(f) + 1)
                else:
                    pe.wait_ge(g_lo_ready, len(GLOW) * c + GLOW.index(f) + 1)
                if f == 0 and static != 0:
                    pe.wait_ge(y_copied, c)
                n = slice((NF + f) * P, (NF + f + 1) * P)
                split_mm(Y[:], w_hi[:, n], w_lo[:, n], g_hi[:, f % HLR, :], g_lo[:, f % HLR, :],
                         start=f == 0, stop=f == NF - 1).then_inc(down_done, 1)

            def turn_y(c):
                pe.wait_ge(y_copied, c + 1)
                for j in range(NT):
                    last = nc.tensor.transpose(T[:, j * P:(j + 1) * P], y_t[:, j * P:(j + 1) * P], ident[:])
                last.then_inc(y_turned, 1)

            def chunk(c, static):
                ahead_too = static != B - 1
                for f in range(NF):
                    if f + LAG < NF:
                        if static != 0 or f != 1:
                            up(c, f + LAG, static == 0)
                    elif ahead_too:
                        up(c + 1, f + LAG - NF, False)
                    if f == 0 and static == 0:
                        turn_weights(0)
                        up(c, f + LAG + 1, True)
                        pe.wait_ge(cwrow_ready, 1)
                        pe.wait_ge(z_act, STEPS)
                        pe.wait_ge(hn_act, STEPS)
                        spread_weights(0, 0)
                        spread_weights(0, 1)
                        pe.wait_ge(pre_ready, STEPS)
                    down(c, f, static)
                    if f == 1 and static != 0:
                        turn_y(c - 1)
                    if f == 0 and static == 0:
                        turn_h(1)
                    if f == 10 and static == 0:
                        turn_h(2)
                    if f == 5 and ahead_too:
                        turn_norm(B + c + 1, 0, MID)
                    if f == 8 and ahead_too:
                        if static == 0:
                            pe.wait_ge(x1_ready, 2)
                        else:
                            pe.wait_ge(y_added, c)
                        logits(c + 1)
                    if f == 15 and static == 0:
                        turn_h(3)
                    if f == 13 and ahead_too:
                        turn_weights(c + 1)

            for k in range(LAST + 1, STEPS - 2):
                body(k, k % B, k)
            turn_h(0, MID)
            body(STEPS - 2, (STEPS - 2) % B, STEPS - 2)

            def first_norm():
                pe.wait_ge(x1_ready, 1)
                turn_norm(B, 0, MID)

            def first_logits():
                pe.wait_ge(in_wg, 16)
                pe.wait_ge(score_ready, STEPS)
                logits(0)

            body(STEPS - 1, (STEPS - 1) % B, STEPS - 1, (None, first_norm, first_logits))
            pe.wait_ge(w_lo_ready, LAST)
            up(0, 0, True)
            up(0, 1, True)
            pe.wait_ge(r_act, STEPS)
            up(0, 2, True)
            up(0, 3, True)
            chunk(0, 0)
            with pe.Fori(1, B - 1) as c:
                chunk(c, None)
            chunk(B - 1, B - 1)
            turn_y(B - 1)


_INS = ['x', 'ctx_1024', 'L0_xattn_Wq', 'L0_xattn_Wk', 'L0_xattn_Wv', 'L0_xattn_gru_wih', 'L0_xattn_gru_whh',
        'L0_xattn_gru_bih', 'L0_xattn_gru_bhh', 'L0_xattn_slot_norm_w', 'L0_xattn_input_norm_w',
        'L0_ffn_Wg', 'L0_ffn_Wu', 'L0_ffn_Wd', 'L0_ffn_W1', 'L0_ffn_W2']
_OUTS = [((4, 512, 128), 'float32')]


def kernel(**inputs):
    import numpy as _np
    import concourse.bacc as _bacc
    from concourse import mybir as _mybir
    from concourse.bass_utils import run_bass_kernel_spmd as _run

    nc = _bacc.Bacc("TRN2", target_bir_lowering=False, num_devices=1)
    arrays, args = {}, []
    for name in _INS:
        a = _np.ascontiguousarray(inputs[name])
        arrays[f"in_{name}_dram"] = a
        args.append(nc.dram_tensor(f"in_{name}_dram", a.shape, _mybir.dt.from_np(a.dtype), kind="ExternalInput").ap())
    for i, (shape, dtype) in enumerate(_OUTS):
        dt = _mybir.dt.from_np(_np.dtype(dtype))
        args.append(nc.dram_tensor(f"out_{i}_dram", shape, dt, kind="ExternalOutput").ap())
    slot_attention_moe_kernel(nc, *args)
    r = _run(nc, [arrays], core_ids=[0])
    return r.results[0]["out_0_dram"]
```
